# Optimizing a Trainium2 kernel written in Bass

```python
import numpy as np
import jax
import jax.numpy as jnp

def _softmax(x, axis=-1):
    return jax.nn.softmax(x, axis=axis)

def _gelu(x):
    return jax.nn.gelu(x, approximate=True)

def _silu(x):
    return jax.nn.silu(x)

def _sigmoid(x):
    return jax.nn.sigmoid(x)

def _layernorm(x, axis=-1, eps=1e-05):
    m = jnp.mean(x, axis=axis, keepdims=True)
    v = jnp.var(x, axis=axis, keepdims=True)
    return (x - m) / jnp.sqrt(v + eps)

def _scatter_add(tgt, idx, src, axis=0):
    return tgt.at[idx].add(src)

def _segment_sum(src, seg, n):
    return jax.ops.segment_sum(src, seg, n)
kernel_name = 'mk_xattn_ffn_d2_seqx_r8_addca5'

def setup_inputs(seed: int=0):
    np.random.seed(seed)
    _w = jnp.asarray

    def _rec_inputs():
        import jax
        import jax.numpy as jnp
        _rk = jax.random.key(seed)
        x = 7.22e-05 + 1 * jax.random.normal(jax.random.fold_in(_rk, 1), (2, 256, 256), jnp.float32)
        _lenS = 256 - jax.random.randint(jax.random.fold_in(_rk, 7), (2,), 0, max(1, 256 // 4) + 1, jnp.int32)
        _lenS2 = 512 - jax.random.randint(jax.random.fold_in(_rk, 8), (2,), 0, max(1, 512 // 4) + 1, jnp.int32)
        _ctx_2048P = jax.random.normal(jax.random.fold_in(_rk, 11), (2, 16, 256), jnp.float32)
        _ctx_2048c = jax.random.dirichlet(jax.random.fold_in(_rk, 511), 0.3 * jnp.ones((16,), jnp.float32), (2, 512))
        _ctx_2048t = jnp.einsum('bsk,bkd->bsd', _ctx_2048c, _ctx_2048P)
        _ctx_2048t = _ctx_2048t * jax.lax.rsqrt(jnp.mean(jnp.square(_ctx_2048t)) + 1e-12) * 0.953939
        ctx_2048 = -0.000514642 + 1.00011 * (_ctx_2048t + 0.3 * jax.random.normal(jax.random.fold_in(_rk, 611), (2, 512, 256), jnp.float32))
        return (x, ctx_2048)
    x, ctx_2048 = _rec_inputs()

    def _L0_xattn_setup():
        import jax, jax.numpy as jnp
        import numpy as np
        HIDDEN = 256
        NUM_HEADS = 16
        NUM_KV_HEADS = 4
        HEAD_DIM = 128
        ROPE_THETA = 10000.0
        EPS = 1e-06

        def rms_norm(x, w, eps=EPS):
            var = jnp.mean(jnp.square(x), axis=-1, keepdims=True)
            return x * jax.lax.rsqrt(var + eps) * w

        def rope_cache(L, head_dim, theta, dtype):
            inv_freq = 1.0 / theta ** (jnp.arange(0, head_dim, 2, dtype=jnp.float32) / head_dim)
            t = jnp.arange(L, dtype=jnp.float32)
            freqs = jnp.outer(t, inv_freq)
            emb = jnp.concatenate([freqs, freqs], -1)
            cos = jnp.cos(emb).astype(dtype)[None, :, None, :]
            sin = jnp.sin(emb).astype(dtype)[None, :, None, :]
            return (cos, sin)

        def rotate_half(x):
            x1, x2 = jnp.split(x, 2, axis=-1)
            return jnp.concatenate([-x2, x1], axis=-1)
        key = jax.random.key(seed)
        ks = jax.random.split(key, 10)
        B, L, T = (2, 256, 64)
        q_out = NUM_HEADS * HEAD_DIM
        kv_out = NUM_KV_HEADS * HEAD_DIM
        s = lambda fan_in: 1.0 / np.sqrt(fan_in)
        return {'x': jax.random.normal(ks[0], (B, L, HIDDEN), jnp.float32), 'h_ctx_kv': jax.random.normal(ks[1], (B, T, HIDDEN), jnp.float32), 'wq': jax.random.normal(ks[2], (HIDDEN, q_out), jnp.float32) * s(HIDDEN), 'wk': jax.random.normal(ks[3], (HIDDEN, kv_out), jnp.float32) * s(HIDDEN), 'wv': jax.random.normal(ks[4], (HIDDEN, kv_out), jnp.float32) * s(HIDDEN), 'wo': jax.random.normal(ks[5], (q_out, HIDDEN), jnp.float32) * s(q_out), 'wk_ctx': jax.random.normal(ks[6], (HIDDEN, kv_out), jnp.float32) * s(HIDDEN), 'wv_ctx': jax.random.normal(ks[7], (HIDDEN, kv_out), jnp.float32) * s(HIDDEN), 'q_norm_w': jnp.ones((HEAD_DIM,), jnp.float32), 'k_norm_w': jnp.ones((HEAD_DIM,), jnp.float32)}
    _L0_xattn_all = _L0_xattn_setup()
    _L0_xattn_in = {k: v for k, v in _L0_xattn_all.items() if k in ('wq', 'wk', 'wv', 'wo', 'wk_ctx', 'wv_ctx', 'q_norm_w', 'k_norm_w')}
    del _L0_xattn_all

    def _L0_ffn_setup():
        import jax, jax.numpy as jnp
        import numpy as np
        D_MODEL = 256
        MLP_RATIO = 4
        TOP_K = 2
        N_EXPERTS = 8
        D_INT = D_MODEL * MLP_RATIO // TOP_K
        BATCH, SEQ = (2, 512)
        key = jax.random.key(seed)
        kx, kr, ki, ko = jax.random.split(key, 4)
        x = jax.random.normal(kx, (BATCH, SEQ, D_MODEL), dtype=jnp.float32)
        Wr = jax.random.normal(kr, (N_EXPERTS, D_MODEL), dtype=jnp.float32) * 0.02
        Win = jax.random.normal(ki, (N_EXPERTS, D_INT, D_MODEL), dtype=jnp.float32) * 0.02
        Wout = jax.random.normal(ko, (N_EXPERTS, D_MODEL, D_INT), dtype=jnp.float32) * 0.02
        return {'x': x, 'Wr': Wr, 'Win': Win, 'Wout': Wout}
    _L0_ffn_all = _L0_ffn_setup()
    _L0_ffn_in = {k: v for k, v in _L0_ffn_all.items() if k in ('Wr', 'Win', 'Wout')}
    del _L0_ffn_all

    def _L1_xattn_setup():
        import jax, jax.numpy as jnp
        import numpy as np
        FP8_MAX = 448.0
        EPS = 1e-05

        def _fp8_roundtrip(x):
            return x.astype(jnp.float8_e4m3fn).astype(jnp.float32)

        def _div_clamp_fp8(x, scale):
            y = jnp.clip(x.astype(jnp.float32) / scale, -FP8_MAX, FP8_MAX)
            y = y.astype(jnp.bfloat16).astype(jnp.float32)
            return _fp8_roundtrip(y)

        def _ln(x, w, b):
            mu = jnp.mean(x, axis=-1, keepdims=True)
            var = jnp.mean(jnp.square(x - mu), axis=-1, keepdims=True)
            return (x - mu) * jax.lax.rsqrt(var + EPS) * w + b

        def _fp8_linear_pertensor(x, wq, w_scale, in_scale):
            xq = _div_clamp_fp8(x, in_scale)
            return jnp.einsum('bsi,oi->bso', xq * in_scale, wq) * w_scale

        def _gqa(q, k, v):
            scale = 1.0 / np.sqrt(q.shape[-1])
            scores = jnp.einsum('bsghd,btgd->bghst', q, k) * scale
            p = jax.nn.softmax(scores, axis=-1)
            return jnp.einsum('bghst,btgd->bsghd', p, v)
        key = jax.random.key(seed)
        ks = jax.random.split(key, 8)
        B, S, SC, H, NH, G, D = (2, 256, 64, 256, 16, 8, 128)

        def qw(k, out_f, in_f):
            w = jax.random.normal(k, (out_f, in_f), jnp.float32) * 0.02
            sc = jnp.max(jnp.abs(w)) / FP8_MAX
            return (_fp8_roundtrip(w / sc), sc.astype(jnp.float32))
        wq, wq_s = qw(ks[0], NH * D, H)
        wqx, wqx_s = qw(ks[1], NH * D, H)
        wk, wk_s = qw(ks[2], G * D, H)
        wv, wv_s = qw(ks[3], G * D, H)
        wproj, wp_s = qw(ks[4], H, 2 * NH * D)
        return {'hidden_states': jax.random.normal(ks[5], (B, S, H), jnp.float32), 'cond': jax.random.normal(ks[6], (B, SC, H), jnp.float32), 'ln_w': jnp.ones((H,), jnp.float32), 'ln_b': jnp.zeros((H,), jnp.float32), 'wq': wq, 'wq_scale': wq_s, 'q_in_scale': jnp.full((H,), 0.05, jnp.float32), 'wqx': wqx, 'wqx_scale': wqx_s, 'qx_in_scale': jnp.full((H,), 0.05, jnp.float32), 'wk': wk, 'wk_scale': wk_s, 'k_in_scale': jnp.full((H,), 0.05, jnp.float32), 'wv': wv, 'wv_scale': wv_s, 'v_in_scale': jnp.full((H,), 0.05, jnp.float32), 'w_kv_x': jax.random.normal(ks[7], (2 * G * D, H), jnp.float32) * 0.02, 'qln_w': jnp.ones((D,), jnp.float32), 'qln_b': jnp.zeros((D,), jnp.float32), 'kln_w': jnp.ones((D,), jnp.float32), 'kln_b': jnp.zeros((D,), jnp.float32), 'qxln_w': jnp.ones((D,), jnp.float32), 'qxln_b': jnp.zeros((D,), jnp.float32), 'kxln_w': jnp.ones((D,), jnp.float32), 'kxln_b': jnp.zeros((D,), jnp.float32), 'wproj': wproj, 'proj_w_scale': wp_s, 'proj_in_scale': jnp.asarray(0.05, jnp.float32), 'proj_smooth': jnp.full((2 * NH * D,), 0.05, jnp.float32)}
    _L1_xattn_all = _L1_xattn_setup()
    _L1_xattn_in = {k: v for k, v in _L1_xattn_all.items() if k in ('ln_w', 'ln_b', 'wq', 'wq_scale', 'q_in_scale', 'wqx', 'wqx_scale', 'qx_in_scale', 'wk', 'wk_scale', 'k_in_scale', 'wv', 'wv_scale', 'v_in_scale', 'w_kv_x', 'qln_w', 'qln_b', 'kln_w', 'kln_b', 'qxln_w', 'qxln_b', 'kxln_w', 'kxln_b', 'wproj', 'proj_w_scale', 'proj_in_scale', 'proj_smooth')}
    del _L1_xattn_all

    def _L1_ffn_setup():
        import jax, jax.numpy as jnp
        import numpy as np
        TOP_K = 8
        NEG_INF = -1000000000.0
        key = jax.random.key(seed)
        ks = jax.random.split(key, 6)
        B, S, H, I, E, G, GS = (1, 256, 256, 176, 64, 8, 8)
        sc = 0.02
        return {'hidden_states': jax.random.normal(ks[0], (B, S, H), jnp.float32), 'gate_w': jax.random.normal(ks[1], (E, H), jnp.float32) * sc, 'mask_up_w': jax.random.normal(ks[2], (G, H, GS), jnp.float32) * sc, 'gate_proj_w': jax.random.normal(ks[3], (G, I, H), jnp.float32) * sc, 'up_proj_w': jax.random.normal(ks[4], (G, I, H), jnp.float32) * sc, 'down_proj_w': jax.random.normal(ks[5], (G, H, I), jnp.float32) * sc, 'inv_map': jnp.arange(G * GS, dtype=jnp.int64).reshape(G, GS)}
    _L1_ffn_all = _L1_ffn_setup()
    _L1_ffn_in = {k: v for k, v in _L1_ffn_all.items() if k in ('gate_w', 'mask_up_w', 'gate_proj_w', 'up_proj_w', 'down_proj_w', 'inv_map')}
    del _L1_ffn_all
    return {'x': x, 'ctx_2048': ctx_2048, 'L0_xattn_wq': _L0_xattn_in['wq'], 'L0_xattn_wk': _L0_xattn_in['wk'], 'L0_xattn_wv': _L0_xattn_in['wv'], 'L0_xattn_wo': _L0_xattn_in['wo'], 'L0_xattn_wk_ctx': _L0_xattn_in['wk_ctx'], 'L0_xattn_wv_ctx': _L0_xattn_in['wv_ctx'], 'L0_xattn_q_norm_w': _L0_xattn_in['q_norm_w'], 'L0_xattn_k_norm_w': _L0_xattn_in['k_norm_w'], 'L0_ffn_Wr': _L0_ffn_in['Wr'], 'L0_ffn_Win': _L0_ffn_in['Win'], 'L0_ffn_Wout': _L0_ffn_in['Wout'], 'L1_xattn_ln_w': _L1_xattn_in['ln_w'], 'L1_xattn_ln_b': _L1_xattn_in['ln_b'], 'L1_xattn_wq': _L1_xattn_in['wq'], 'L1_xattn_wq_scale': _L1_xattn_in['wq_scale'], 'L1_xattn_q_in_scale': _L1_xattn_in['q_in_scale'], 'L1_xattn_wqx': _L1_xattn_in['wqx'], 'L1_xattn_wqx_scale': _L1_xattn_in['wqx_scale'], 'L1_xattn_qx_in_scale': _L1_xattn_in['qx_in_scale'], 'L1_xattn_wk': _L1_xattn_in['wk'], 'L1_xattn_wk_scale': _L1_xattn_in['wk_scale'], 'L1_xattn_k_in_scale': _L1_xattn_in['k_in_scale'], 'L1_xattn_wv': _L1_xattn_in['wv'], 'L1_xattn_wv_scale': _L1_xattn_in['wv_scale'], 'L1_xattn_v_in_scale': _L1_xattn_in['v_in_scale'], 'L1_xattn_w_kv_x': _L1_xattn_in['w_kv_x'], 'L1_xattn_qln_w': _L1_xattn_in['qln_w'], 'L1_xattn_qln_b': _L1_xattn_in['qln_b'], 'L1_xattn_kln_w': _L1_xattn_in['kln_w'], 'L1_xattn_kln_b': _L1_xattn_in['kln_b'], 'L1_xattn_qxln_w': _L1_xattn_in['qxln_w'], 'L1_xattn_qxln_b': _L1_xattn_in['qxln_b'], 'L1_xattn_kxln_w': _L1_xattn_in['kxln_w'], 'L1_xattn_kxln_b': _L1_xattn_in['kxln_b'], 'L1_xattn_wproj': _L1_xattn_in['wproj'], 'L1_xattn_proj_w_scale': _L1_xattn_in['proj_w_scale'], 'L1_xattn_proj_in_scale': _L1_xattn_in['proj_in_scale'], 'L1_xattn_proj_smooth': _L1_xattn_in['proj_smooth'], 'L1_ffn_gate_w': _L1_ffn_in['gate_w'], 'L1_ffn_mask_up_w': _L1_ffn_in['mask_up_w'], 'L1_ffn_gate_proj_w': _L1_ffn_in['gate_proj_w'], 'L1_ffn_up_proj_w': _L1_ffn_in['up_proj_w'], 'L1_ffn_down_proj_w': _L1_ffn_in['down_proj_w'], 'L1_ffn_inv_map': _L1_ffn_in['inv_map']}

def reference(x, ctx_2048, L0_xattn_wq, L0_xattn_wk, L0_xattn_wv, L0_xattn_wo, L0_xattn_wk_ctx, L0_xattn_wv_ctx, L0_xattn_q_norm_w, L0_xattn_k_norm_w, L0_ffn_Wr, L0_ffn_Win, L0_ffn_Wout, L1_xattn_ln_w, L1_xattn_ln_b, L1_xattn_wq, L1_xattn_wq_scale, L1_xattn_q_in_scale, L1_xattn_wqx, L1_xattn_wqx_scale, L1_xattn_qx_in_scale, L1_xattn_wk, L1_xattn_wk_scale, L1_xattn_k_in_scale, L1_xattn_wv, L1_xattn_wv_scale, L1_xattn_v_in_scale, L1_xattn_w_kv_x, L1_xattn_qln_w, L1_xattn_qln_b, L1_xattn_kln_w, L1_xattn_kln_b, L1_xattn_qxln_w, L1_xattn_qxln_b, L1_xattn_kxln_w, L1_xattn_kxln_b, L1_xattn_wproj, L1_xattn_proj_w_scale, L1_xattn_proj_in_scale, L1_xattn_proj_smooth, L1_ffn_gate_w, L1_ffn_mask_up_w, L1_ffn_gate_proj_w, L1_ffn_up_proj_w, L1_ffn_down_proj_w, L1_ffn_inv_map):
    import jax
    import jax.numpy as jnp

    def _L0_xattn_ref(x, h_ctx_kv, wq, wk, wv, wo, wk_ctx, wv_ctx, q_norm_w, k_norm_w):
        import jax, jax.numpy as jnp
        import numpy as np
        HIDDEN = 256
        NUM_HEADS = 16
        NUM_KV_HEADS = 4
        HEAD_DIM = 128
        ROPE_THETA = 10000.0
        EPS = 1e-06

        def rms_norm(x, w, eps=EPS):
            var = jnp.mean(jnp.square(x), axis=-1, keepdims=True)
            return x * jax.lax.rsqrt(var + eps) * w

        def rope_cache(L, head_dim, theta, dtype):
            inv_freq = 1.0 / theta ** (jnp.arange(0, head_dim, 2, dtype=jnp.float32) / head_dim)
            t = jnp.arange(L, dtype=jnp.float32)
            freqs = jnp.outer(t, inv_freq)
            emb = jnp.concatenate([freqs, freqs], -1)
            cos = jnp.cos(emb).astype(dtype)[None, :, None, :]
            sin = jnp.sin(emb).astype(dtype)[None, :, None, :]
            return (cos, sin)

        def rotate_half(x):
            x1, x2 = jnp.split(x, 2, axis=-1)
            return jnp.concatenate([-x2, x1], axis=-1)
        B, L, _ = x.shape
        T = h_ctx_kv.shape[1]
        rep = NUM_HEADS // NUM_KV_HEADS
        q = (x @ wq).reshape(B, L, NUM_HEADS, HEAD_DIM)
        k = (x @ wk).reshape(B, L, NUM_KV_HEADS, HEAD_DIM)
        v = (x @ wv).reshape(B, L, NUM_KV_HEADS, HEAD_DIM)
        q = rms_norm(q, q_norm_w)
        k = rms_norm(k, k_norm_w)
        k_ctx = (h_ctx_kv @ wk_ctx).reshape(B, T, NUM_KV_HEADS, HEAD_DIM)
        v_ctx = (h_ctx_kv @ wv_ctx).reshape(B, T, NUM_KV_HEADS, HEAD_DIM)
        k_ctx = rms_norm(k_ctx, k_norm_w)
        cos, sin = rope_cache(L, HEAD_DIM, ROPE_THETA, x.dtype)
        q = q * cos + rotate_half(q) * sin
        k = k * cos + rotate_half(k) * sin
        k_full = jnp.concatenate([k_ctx, k], axis=1)
        v_full = jnp.concatenate([v_ctx, v], axis=1)
        k_full = jnp.repeat(k_full, rep, axis=2)
        v_full = jnpp_repeat = jnp.repeat(v_full, rep, axis=2)
        i = jnp.arange(L)[:, None]
        j = jnp.arange(L)[None, :]
        causal = jnp.where(j > i, -jnp.inf, 0.0).astype(x.dtype)
        mask = jnp.concatenate([jnp.zeros((L, T), x.dtype), causal], axis=1)
        scale = 1.0 / np.sqrt(HEAD_DIM)
        scores = jnp.einsum('blhd,bmhd->bhlm', q, k_full) * scale + mask
        probs = jax.nn.softmax(scores, axis=-1)
        out = jnp.einsum('bhlm,bmhd->blhd', probs, v_full)
        out = out.reshape(B, L, NUM_HEADS * HEAD_DIM)
        return out @ wo

    def _L0_ffn_ref(x, Wr, Win, Wout):
        import jax, jax.numpy as jnp
        import numpy as np
        D_MODEL = 256
        MLP_RATIO = 4
        TOP_K = 2
        N_EXPERTS = 8
        D_INT = D_MODEL * MLP_RATIO // TOP_K
        BATCH, SEQ = (2, 512)
        orig_shape = x.shape
        xf = x.reshape(-1, orig_shape[-1])
        T = xf.shape[0]
        logits = xf @ Wr.T
        scores, expert = jax.lax.top_k(logits, TOP_K)
        weights = jax.nn.softmax(scores, axis=-1)
        gate = jnp.zeros((T, N_EXPERTS), dtype=xf.dtype)
        gate = gate.at[jnp.arange(T)[:, None], expert].add(weights)
        y = jnp.zeros_like(xf)
        for e in range(N_EXPERTS):
            h = jax.nn.silu(xf @ Win[e].T)
            y = y + gate[:, e:e + 1] * (h @ Wout[e].T)
        return y.reshape(orig_shape)

    def _L1_xattn_ref(hidden_states, cond, ln_w, ln_b, wq, wq_scale, q_in_scale, wqx, wqx_scale, qx_in_scale, wk, wk_scale, k_in_scale, wv, wv_scale, v_in_scale, w_kv_x, qln_w, qln_b, kln_w, kln_b, qxln_w, qxln_b, kxln_w, kxln_b, wproj, proj_w_scale, proj_in_scale, proj_smooth):
        import jax, jax.numpy as jnp
        import numpy as np
        FP8_MAX = 448.0
        EPS = 1e-05

        def _fp8_roundtrip(x):
            return x.astype(jnp.float8_e4m3fn).astype(jnp.float32)

        def _div_clamp_fp8(x, scale):
            y = jnp.clip(x.astype(jnp.float32) / scale, -FP8_MAX, FP8_MAX)
            y = y.astype(jnp.bfloat16).astype(jnp.float32)
            return _fp8_roundtrip(y)

        def _ln(x, w, b):
            mu = jnp.mean(x, axis=-1, keepdims=True)
            var = jnp.mean(jnp.square(x - mu), axis=-1, keepdims=True)
            return (x - mu) * jax.lax.rsqrt(var + EPS) * w + b

        def _fp8_linear_pertensor(x, wq, w_scale, in_scale):
            xq = _div_clamp_fp8(x, in_scale)
            return jnp.einsum('bsi,oi->bso', xq * in_scale, wq) * w_scale

        def _gqa(q, k, v):
            scale = 1.0 / np.sqrt(q.shape[-1])
            scores = jnp.einsum('bsghd,btgd->bghst', q, k) * scale
            p = jax.nn.softmax(scores, axis=-1)
            return jnp.einsum('bghst,btgd->bsghd', p, v)
        b, s, _ = hidden_states.shape
        sc = cond.shape[1]
        d = qln_w.shape[0]
        nh = wq.shape[0] // d
        g = wk.shape[0] // d
        hpg = nh // g
        ln_out = _ln(hidden_states, ln_w, ln_b)
        q = _fp8_linear_pertensor(ln_out, wq, wq_scale, q_in_scale).reshape(b, s, g, hpg, d)
        q = _ln(q, qln_w, qln_b)
        k = _fp8_linear_pertensor(ln_out, wk, wk_scale, k_in_scale).reshape(b, s, g, d)
        k = _ln(k, kln_w, kln_b)
        v = _fp8_linear_pertensor(ln_out, wv, wv_scale, v_in_scale).reshape(b, s, g, d)
        core = _gqa(q, k, v).reshape(b, s, nh * d)
        qx = _fp8_linear_pertensor(ln_out, wqx, wqx_scale, qx_in_scale).reshape(b, s, g, hpg, d)
        qx = _ln(qx, qxln_w, qxln_b)
        kvx = jnp.einsum('bsi,oi->bso', cond, w_kv_x)
        kx, vx = jnp.split(kvx, 2, axis=-1)
        kx = _ln(kx.reshape(b, sc, g, d), kxln_w, kxln_b)
        vx = vx.reshape(b, sc, g, d)
        xout = _gqa(qx, kx, vx).reshape(b, s, nh * d)
        cat = jnp.concatenate([core, xout], axis=-1)
        catq = _div_clamp_fp8(cat, proj_smooth)
        return jnp.einsum('bsi,oi->bso', catq, wproj) * (proj_in_scale * proj_w_scale)

    def _L1_ffn_ref(hidden_states, gate_w, mask_up_w, gate_proj_w, up_proj_w, down_proj_w, inv_map):
        import jax, jax.numpy as jnp
        import numpy as np
        TOP_K = 8
        NEG_INF = -1000000000.0
        B, S, H = hidden_states.shape
        x = hidden_states.reshape(-1, H)
        N = x.shape[0]
        E = gate_w.shape[0]
        scores = jax.nn.softmax(x @ gate_w.T, axis=-1)
        topk_w, topk_idx = jax.lax.top_k(scores, TOP_K)
        w_e = jnp.zeros((N, E), x.dtype).at[jnp.arange(N)[:, None], topk_idx].add(topk_w)
        flat = w_e[:, inv_map]
        scalar = flat.sum(-1)
        soft = jax.nn.softmax(jnp.where(flat == 0, NEG_INF, flat), axis=-1)
        xg = x[:, None, :] + jnp.einsum('ngi,ghi->ngh', soft, mask_up_w)
        g = jnp.einsum('ngh,gih->ngi', xg, gate_proj_w)
        u = jnp.einsum('ngh,gih->ngi', xg, up_proj_w)
        a = jax.nn.silu(g) * u
        d = jnp.einsum('ngi,ghi->ngh', a, down_proj_w)
        y = jnp.einsum('ng,ngh->nh', scalar, d)
        return y.reshape(B, S, H)
    x = x + _L0_xattn_ref(_layernorm(x, axis=-1), ctx_2048, L0_xattn_wq, L0_xattn_wk, L0_xattn_wv, L0_xattn_wo, L0_xattn_wk_ctx, L0_xattn_wv_ctx, L0_xattn_q_norm_w, L0_xattn_k_norm_w)
    x = x + _L0_ffn_ref(_layernorm(x, axis=-1), L0_ffn_Wr, L0_ffn_Win, L0_ffn_Wout)
    x = x + _L1_xattn_ref(_layernorm(x, axis=-1), ctx_2048, L1_xattn_ln_w, L1_xattn_ln_b, L1_xattn_wq, L1_xattn_wq_scale, L1_xattn_q_in_scale, L1_xattn_wqx, L1_xattn_wqx_scale, L1_xattn_qx_in_scale, L1_xattn_wk, L1_xattn_wk_scale, L1_xattn_k_in_scale, L1_xattn_wv, L1_xattn_wv_scale, L1_xattn_v_in_scale, L1_xattn_w_kv_x, L1_xattn_qln_w, L1_xattn_qln_b, L1_xattn_kln_w, L1_xattn_kln_b, L1_xattn_qxln_w, L1_xattn_qxln_b, L1_xattn_kxln_w, L1_xattn_kxln_b, L1_xattn_wproj, L1_xattn_proj_w_scale, L1_xattn_proj_in_scale, L1_xattn_proj_smooth)
    x = x + _L1_ffn_ref(_layernorm(x, axis=-1), L1_ffn_gate_w, L1_ffn_mask_up_w, L1_ffn_gate_proj_w, L1_ffn_up_proj_w, L1_ffn_down_proj_w, L1_ffn_inv_map)
    return x

_drawn_inputs = setup_inputs


def setup_inputs(seed=0):
    import zlib

    import numpy as np

    out = dict(_drawn_inputs(seed))
    spreads = {'L0_xattn_q_norm_w': (1.0, 0.2),
     'L0_xattn_k_norm_w': (1.0, 0.2),
     'L1_xattn_ln_w': (1.0, 0.6),
     'L1_xattn_ln_b': (0.0, 0.289),
     'L1_xattn_q_in_scale': (0.05000000074505806, 0.6),
     'L1_xattn_qx_in_scale': (0.05000000074505806, 0.6),
     'L1_xattn_k_in_scale': (0.05000000074505806, 0.6),
     'L1_xattn_v_in_scale': (0.05000000074505806, 0.6),
     'L1_xattn_qln_w': (1.0, 0.6),
     'L1_xattn_qln_b': (0.0, 0.8),
     'L1_xattn_kln_w': (1.0, 0.6),
     'L1_xattn_kln_b': (0.0, 0.8),
     'L1_xattn_qxln_w': (1.0, 0.6),
     'L1_xattn_qxln_b': (0.0, 0.8),
     'L1_xattn_kxln_w': (1.0, 0.6),
     'L1_xattn_kxln_b': (0.0, 0.8),
     'L1_xattn_proj_smooth': (0.05000000074505806, 0.2)}
    factors = {'L1_ffn_gate_w': 8.0,
     'L1_ffn_mask_up_w': 8.0,
     'L1_ffn_gate_proj_w': 8.0,
     'L1_ffn_up_proj_w': 8.0,
     'L1_ffn_down_proj_w': 8.0}
    for name, (base, spread) in spreads.items():
        noise = np.random.default_rng([zlib.crc32(name.encode()), seed]).standard_normal(out[name].shape)
        drawn = base * np.exp(spread * noise) if base else spread * noise
        out[name] = jnp.asarray(drawn.astype(out[name].dtype))
    for name, factor in factors.items():
        out[name] = (out[name] * factor).astype(out[name].dtype)
    return out
```

```python
from contextlib import ExitStack

import numpy as np
import concourse.bass as bass
from concourse import mybir

F32 = mybir.dt.float32
F32R = mybir.dt.float32r
BF16 = mybir.dt.bfloat16
U16 = mybir.dt.uint16
I32 = mybir.dt.int32
ALU = mybir.AluOpType
ACT = mybir.ActivationFunctionType
AX = mybir.AxisListType

P = 128
T = 512
TT = T // P
H = 256
HC = H // P
NCTX = 1024
CT = NCTX // P
BANK = 512
NEG = -1.0e30

QW, KVW, CKVW, OW, SMW = 2 * 512, 2 * 256, 2 * 256, 4 * 256, 4
CKV0 = 0
KV0 = CKV0 + CKVW
Q0 = KV0 + KVW
O0 = Q0 + QW
SM0 = O0 + OW
GW = SM0 + SMW

E0, D_INT = 8, 512
EUP, EDN = HC * D_INT, (D_INT // P) * H
EW = EUP + EDN
G1, GS, I1 = 8, 8, 176
IH = I1 // 2
G_GATE, G_UP, G_DN, G_MU = 0, HC * I1, 2 * HC * I1, 2 * HC * I1 + 2 * H
FW = G_MU + H
NE1 = G1 * GS

STAGES = 4

V_KNORM, V_QLN, V_QXLN, V_KLN, V_KXLN = 0, 1, 3, 5, 7
V_LN, V_IN, V_WS, V_PS, V_PIDX, V_MH, V_EPS = 9, 13, 21, 25, 27, 28, 29
NV = 31

RMS_EPS, LN_EPS = 1e-6, 1e-5
HEAD_SCALE = float(1.0 / np.sqrt(P))
ROOT_D = float(np.sqrt(P))
FP8_MAX = 448.0
FP8_MIN_NORMAL = 2.0 ** -6
FP8_MAGIC = 1.5 * 2.0 ** 20

ATTN_SEMS = ("w_in kv_in wo_in "
             "proj turned scores pt outt y "
             "w_scaled raw squares t_vec prob pnorm pt_hi o_hi "
             "w_hi wo_hi smooth sums v_hi aggr roped rope_sum norm t_hi rowmax nmax rsum pt_lo "
             "o_clip o_bf o_exp o_magic o_lo x_done "
             "w_lo wo_lo var rstd v_lo t_lo o_add o_q").split()
ONLY = ("squares o_hi roped rope_sum o_lo".split(),
        "kv_in w_scaled smooth aggr o_clip o_bf o_exp o_magic o_add o_q".split())
ORDER = (("P", 0), ("P", 1), ("T", 0), ("P", 2), ("T", 1), ("P", 3), ("T", 2), ("P", 4), ("T", 3), ("T", 4))
FIRST_ORDER = (("P", 0), ("P", 1), ("P", 2), ("T", 0), ("P", 3), ("T", 1), ("P", 4), ("T", 2), ("T", 3), ("T", 4))
PLACES = (((0, 1), (1, 1), (2, 0), (2, 2), (3, 0), (3, 2), (4, 0), (4, 1), (5, 0), (6, 0)),
          ((0, 2), (1, 2), (2, 0), (2, 2), (2, 2), (3, 0), (3, 0), (3, 1), (3, 2), (3, 2)))
Y_PLACES = (((3, 1, 5), (3, 2, 6)), ((3, 1, 8), (3, 2, 10)))


def plan(layer):
    units = (16, 8)[layer]
    for half in range(2):
        for n, (what, k) in enumerate(ORDER):
            for j, (step, place, behind) in enumerate(Y_PLACES[layer]):
                if half == 0 and behind == n:
                    yield step, place, "Y", 0, j
            step, place = PLACES[layer][n]
            yield step + half * units // 2, place, what, half, k
        for j, (step, place, behind) in enumerate(Y_PLACES[layer]):
            if half == 0 and behind == len(ORDER):
                yield step, place, "Y", 0, j


SPLITS = ((3, 6, 7, 5), (1, 4, 4, 5))


NORM_SEMS = "sums aggr var rstd norm turned hi lo vec scaled bf exp magic add q add_dve q_dve".split()
MOE_SEMS = ("w_in0 w_in1 w_hi w_lo logits route route_exp turned flat gates xg xg_sum xg_hi xg_lo "
            "up act prod a_hi a_lo y x_done").split()


def events_of(layer, g, step, first, last, places=(0, 1, 2)):
    for at, place, what, half, k in plan(layer):
        if at != step or place not in places:
            continue
        if what == "Y":
            if not first:
                yield what, (g - 1, k)
        elif not (last and half == 1):
            yield what, (g + half, 1 - half, k)


def steps_of(units, last):
    return range(units + 3 if last else units)


def first_of_all(g, b):
    return isinstance(g, int) and g == 0 and b == 0


def n_par(b, k):
    return (5 * b + k) % 2


def p_bank(g, b, k):
    return k if first_of_all(g, b) else 7


def t_bank(g, b, k):
    return 5 + k % 2 if first_of_all(g, b) else 7


class Split:

    def __init__(self, hi, lo):
        self.hi, self.lo = hi, lo

    def __getitem__(self, at):
        return Split(self.hi[at], self.lo[at])

    def view(self, pattern, **sizes):
        return Split(self.hi.rearrange(pattern, **sizes), self.lo.rearrange(pattern, **sizes))


def f32(ap):
    return ap.bitcast(F32)


def product(nc, out, a, b, start, stop):
    nc.tensor.matmul(out, a.hi, b.hi, start=start, stop=False)
    nc.tensor.matmul(out, a.hi, b.lo, start=False, stop=False)
    return nc.tensor.matmul(out, a.lo, b.hi, start=False, stop=stop)


def product_exact(nc, out, a, b, start, stop):
    nc.tensor.matmul(out, a, b.hi, start=start, stop=False)
    return nc.tensor.matmul(out, a, b.lo, start=False, stop=stop)


def build(nc, x_d, ctx_d, wg_d, we_d, wf_d, vec_d, rows_d, router0_d, router1_d, inv_d, rope_d, mask_d, ident_d,
          desc_d, out_d, stages):
    stack = ExitStack()
    with stack:
        def sb(name, shape, dt=F32):
            return stack.enter_context(nc.sbuf_tensor(name, shape, dt))

        def sem(name):
            return stack.enter_context(nc.semaphore(name))

        X = sb("X", [P, TT, H])
        ctxT = Split(sb("ctx_hi", [P, HC, NCTX], F32R), sb("ctx_lo", [P, HC, NCTX], F32R))
        xT = Split(sb("xT_hi", [P, HC, T], F32R), sb("xT_lo", [P, HC, T], F32R))
        ident = sb("ident", [P, P])
        ident_r = sb("ident_r", [P, P], F32R)
        mask_r = sb("mask_r", [P, 2, 256], F32R)
        rows = sb("rows", [P, 2, P])
        rope_w = sb("rope_w", [P, 2, 2, 2, P])
        vec = sb("vec", [P, NV])
        in_rcp = sb("in_rcp", [P, 8])
        in_ws = sb("in_ws", [P, 8])
        out_ws = sb("out_ws", [P, 1])
        W_raw = sb("W_raw", [P, 2 * EW])
        W = Split(sb("W_hi", [P, 2 * EW], F32R), sb("W_lo", [P, 2 * EW], F32R))
        QT = Split(sb("QT_hi", [P, 4, T], F32R), sb("QT_lo", [P, 4, T], F32R))
        KT = Split(sb("KT_hi", [P, NCTX + T], F32R), sb("KT_lo", [P, NCTX + T], F32R))
        V = Split(sb("V_hi", [P, CT + TT, P], F32R), sb("V_lo", [P, CT + TT, P], F32R))
        PT = Split(sb("PT_hi", [P, 2, 6, 256], F32R), sb("PT_lo", [P, 2, 6, 256], F32R))
        OT = Split(sb("OT_hi", [P, 4, T], F32R), sb("OT_lo", [P, 4, T], F32R))
        prob = sb("prob", [P, 3, 768])
        KN = sb("KN", [P, 2, 1024])
        TV = sb("TV", [P, 2, 1024])
        SQ = sb("SQ", [P, 1024])
        RP = sb("RP", [P, 1024])
        SQB = TV[:, 1, 0:512]
        XN = KN[:, 0, :].rearrange("p (t n) -> p t n", t=TT)
        wide2048 = prob[:, :, :].rearrange("p a n -> p (a n)")[:, 0:2048]
        ctx_raw = wide2048.rearrange("p (c n) -> p c n", c=HC)
        hf = wide2048.rearrange("p (m n) -> p m n", m=4)
        rope = RP[:, 0:512].rearrange("p (k t d) -> p k t d", k=2, t=2)
        mask = RP[:, 512:1024].rearrange("p (t n) -> p t n", t=2)
        RT = [SQ[:, i * TT * NE1:(i + 1) * TT * NE1] for i in range(4)]
        softT = Split(*(a[0:NE1, 0, :, :].rearrange("p k n -> p (k n)")[:, 0:T] for a in (PT.hi, PT.lo)))
        xq = [xT.hi[:, :, :], xT.lo[:, :, :], OT.lo[:, 0:2, :], OT.lo[:, 2:4, :]]
        q_in = [wide2048[:, i * 1024:(i + 1) * 1024] for i in range(2)]
        stat = sb("stat", [P, 8, 6])
        q_ln = sb("q_ln", [P, 4])
        tick = sb("tick", [P, 1])
        mv = sb("mv", [P, 2, 8, 2])
        ssum = sb("ssum", [P, 2, 8])
        vv = sb("vv", [P, 2, 8])
        rr = sb("rr", [P, 2, 8])
        RQ = sb("RQ", [P, 16])
        MX = sb("MX", [P, 4, 2])
        NM = sb("NM", [P, 4, 2])
        SM = sb("SM", [P, 4, 2])
        RC = sb("RC", [P, 4, 2])
        srs = sb("srs", [P, 4])
        QY = sb("QY", [P, 1024], BF16)
        QE = sb("QE", [P, 1024], BF16)
        QY1 = sb("QY1", [P, 1024], BF16)
        q_bf, q_magic, q_sum = [QY[:, :], QY1[:, :]], [RP[:, :], KN[:, 1, :]], [KN[:, 0, :], SQ[:, :]]
        ln_v = sb("ln_v", [P, TT])
        gate0 = sb("gate0", [P, TT, E0])
        r0 = Split(sb("r0_hi", [P, HC, E0], F32R), sb("r0_lo", [P, HC, E0], F32R))
        r1 = Split(sb("r1_hi", [P, HC, NE1], F32R), sb("r1_lo", [P, HC, NE1], F32R))
        r0_raw = sb("r0_raw", [P, HC, E0])
        r1_raw = sb("r1_raw", [P, HC, NE1])
        inv = sb("inv", [NE1, NE1], I32)
        perm = sb("perm", [NE1, NE1])
        RS = sb("RS", [P, 8, 32])
        scal1 = sb("scal1", [P, TT, G1])
        top8 = sb("top8", [P, TT, 8])
        PS = stack.enter_context(nc.psum_tensor("PS", [P, 8 * BANK], F32))

        def bank(n, width=BANK, rows=P):
            return PS[0:rows, n * BANK:n * BANK + width]

        loaded = sem("loaded")
        ctx_loaded = sem("ctx_loaded")
        ctx_hi = sem("ctx_hi_ready")
        ctx_lo = sem("ctx_lo_ready")
        consts = sem("consts")
        stored = sem("stored")
        LOADS = 7
        layers = [{n: sem(f"attn{i}_{n}") for n in ATTN_SEMS if n not in ONLY[1 - i]} for i in range(2)]
        x_loaded = sem("x_loaded")
        vec_loaded = sem("vec_loaded")
        ident_loaded = sem("ident_loaded")
        first_q_in = sem("first_q_in")
        norm_sems = {n: sem(f"norm_{n}") for n in NORM_SEMS}
        norms = [{"nth": i + 1, "nth_turn": (1, 2, 0, 3, 4)[i], "nth_split": (1, 2, 0, 0, 3)[i],
                  "nth_vec": (0, 0, 0, 1, 2)[i], **norm_sems} for i in range(5)]
        moes = [{n: sem(f"moe{i}_{n}") for n in MOE_SEMS} for i in range(2)]
        x_ready = [None, (layers[0]["x_done"], 2 * 4 + 1), (moes[0]["x_done"], E0 + 1), (layers[1]["x_done"], 2 * 8 + 1),
                   (moes[1]["x_done"], G1 + 1)]
        N_CONSTS = 16

        blk = stack.enter_context(nc.Block())

        def each(engine, n, body):
            with engine.Fori(0, n - 1) as g:
                body(g, False)
            body(n - 1, True)

        def each_group(engine, n, body):
            body(0, True, False)
            with engine.Fori(1, n - 1) as g:
                body(g, False, False)
            body(n - 1, False, True)

        @blk.sync
        def _(sp):
            sp.dma_start(X[:, :, :], x_d).then_inc(x_loaded, 16)
            sp.dma_start(vec[:, :], vec_d).then_inc(vec_loaded, 16)
            sp.dma_start(ident[:, :], ident_d).then_inc(ident_loaded, 16)
            sp.dma_start(W_raw[:, Q0:O0], wg_d[0, :, Q0:O0]).then_inc(first_q_in, 16)
            sp.dma_start(W_raw[:, 0:Q0], wg_d[0, :, 0:Q0]).then_inc(layers[0]["w_in"], 16)
            sp.dma_start(ctx_raw[:, :, :], ctx_d).then_inc(ctx_loaded, 16)
            for t, d in ((rows[:, :, :], rows_d), (rope[:, :, :, :], rope_d),
                         (mask[:, :, :], mask_d), (r0_raw[:, :, :], router0_d), (r1_raw[:, :, :], router1_d),
                         (inv[:, :], inv_d), (RS[:, 7, 0:8], desc_d)):
                sp.dma_start(t, d).then_inc(loaded, 16)
            sp.dma_start(W_raw[:, O0:GW], wg_d[0, :, O0:GW]).then_inc(layers[0]["wo_in"], 16)

            def qkv_in(L, li, n):
                if li == 0:
                    sp.dma_start(W_raw[:, 0:O0], wg_d[n, :, 0:O0]).then_inc(L["w_in"], 16)
                else:
                    sp.dma_start(W_raw[:, Q0:O0], wg_d[n, :, Q0:O0]).then_inc(L["w_in"], 16)
                    sp.dma_start(W_raw[:, 0:KV0], wg_d[n, :, 0:KV0]).then_inc(L["w_in"], 16)

            def attention(li, groups, first):
                L = layers[li]

                def body(g, last):
                    sp.wait_ge(L["w_lo"], 3 * g + 3 if li == 0 else 2 * g + 2)
                    if not last:
                        qkv_in(L, li, g + (first + 1))
                    if li == 1:
                        sp.wait_ge(L["proj"], 10 * g + 8)
                        if not last:
                            sp.dma_start(W_raw[:, KV0:Q0], wg_d[g + (first + 1), :, KV0:Q0]).then_inc(L["kv_in"], 16)
                    sp.wait_ge(L["wo_lo"], g + 1)
                    if li == 1:
                        sp.wait_ge(L["smooth"], g + 1)
                    if not last:
                        sp.dma_start(W_raw[:, O0:GW], wg_d[g + (first + 1), :, O0:GW]).then_inc(L["wo_in"], 16)
                each(nc.sync, groups, body)

            def moe(li, w_d, n, width):
                M = moes[li]
                sp.dma_start(W_raw[:, 0:width], w_d[0]).then_inc(M["w_in0"], 16)
                sp.dma_start(W_raw[:, EW:EW + width], w_d[1]).then_inc(M["w_in1"], 16)
                def body(i, last):
                    for j in range(2):
                        sp.wait_ge(M["w_lo"], 2 * i + j + 1)
                        if not last:
                            sp.dma_start(W_raw[:, j * EW:j * EW + width], w_d[2 * i + (j + 2)])\
                              .then_inc((M["w_in0"], M["w_in1"])[j], 16)
                each(nc.sync, n // 2, body)

            attention(0, 4, 0)
            if stages >= 2:
                moe(0, we_d, E0, EW)
            if stages >= 3:
                qkv_in(layers[1], 1, 4)
                sp.dma_start(W_raw[:, KV0:Q0], wg_d[4, :, KV0:Q0]).then_inc(layers[1]["kv_in"], 16)
                sp.dma_start(W_raw[:, O0:GW], wg_d[4, :, O0:GW]).then_inc(layers[1]["wo_in"], 16)
                attention(1, 8, 4)
            if stages >= 4:
                moe(1, wf_d, G1, FW)
            s, v = x_ready[stages]
            sp.wait_ge(s, v)
            sp.dma_start(out_d, X[:, :, :]).then_inc(stored, 16)
            sp.wait_ge(stored, 16)

        @blk.tensor
        def _(pe):
            def turn_rows(N):
                pe.wait_ge(N["norm"], N["nth"])
                for c in range(HC):
                    for t in range(TT):
                        last = nc.tensor.transpose(PS[:, (4 + c) * BANK + t * P:(4 + c) * BANK + (t + 1) * P],
                                                   XN[:, t, c * P:(c + 1) * P], ident[:, :])
                last.then_inc(N["turned"], 1)

            def project(li, g, b, k):
                L, layer1 = layers[li], li == 1
                n = g * 10 + 5 * b + k
                if not layer1:
                    pe.wait_ge(L["w_lo"], 3 * g + (1, 1, 2, 3, 3)[k])
                elif k == 2:
                    pe.wait_ge(L["w_scaled"], 2 * g + 2)
                else:
                    pe.wait_ge(L["w_lo"], 2 * g + (1, 1, 0, 2, 2)[k])
                if first_of_all(g, b):
                    pass
                elif k == 1:
                    pe.wait_ge(L["raw"], n)
                elif k >= 2:
                    pe.wait_ge(L["t_vec"], n - 1)
                else:
                    pe.wait_ge(L["t_vec"], n)
                at = p_bank(g, b, k) * BANK
                if k < 2:
                    tiles, width, w0 = (2 * b + k,), 512, Q0
                elif k == 2:
                    tiles, width, w0 = (2 * b, 2 * b + 1), 256, KV0
                else:
                    tiles, width, w0 = (b * 4 + 2 * k - 6, b * 4 + 2 * k - 5), 256, CKV0
                for t in tiles:
                    tok = slice(t * P, (t + 1) * P)
                    if layer1 and k < 3:
                        half, a0 = width // 2, 2 if k == 2 else 0
                        for j in range(2):
                            for c in range(HC):
                                cols = slice(w0 + (2 * c + j) * half, w0 + (2 * c + j + 1) * half)
                                out, a = PS[:, at:at + half], xq[a0 + j][:, c, tok]
                                if k == 2:
                                    last = nc.tensor.matmul(out, f32(a), W_raw[:, cols], start=c == 0,
                                                            stop=c == HC - 1)
                                else:
                                    last = product_exact(nc, out, a, W[:, cols], c == 0, c == HC - 1)
                            at += half
                        continue
                    a = ctxT if k >= 3 else xT
                    for c in range(HC):
                        last = product(nc, PS[:, at:at + width], a[:, c, tok],
                                       W[:, w0 + c * width:w0 + (c + 1) * width], c == 0, c == HC - 1)
                    at += width
                last.then_inc(L["proj"], 1)

            def turn(li, g, b, k):
                L = layers[li]
                n = g * 10 + 5 * b + k
                pe.wait_ge(L["norm"], n + 1)
                if first_of_all(g, b):
                    if k >= 2:
                        pe.wait_ge(L["t_vec"], k - 1)
                elif k < 4:
                    pe.wait_ge(L["raw"], n + 2)
                else:
                    pe.wait_ge(L["t_vec"], n)
                at = t_bank(g, b, k) * BANK
                for m in range(4 if k < 2 else 2):
                    last = nc.tensor.transpose(PS[:, at + m * P:at + (m + 1) * P],
                                               KN[:, 0, (n_par(b, k) * 4 + m) * P:(n_par(b, k) * 4 + m + 1) * P],
                                               ident[:, :])
                last.then_inc(L["turned"], 1)

            def output(li, g, half):
                L, layer1 = layers[li], li == 1
                pairs = 4 if layer1 else 8
                pe.wait_ge(L["wo_lo"], g + 1)
                if half == 0:
                    pe.wait_ge(L["o_q"] if layer1 else L["o_lo"], g * pairs + pairs)
                else:
                    pe.wait_ge(L["x_done"], 2 * g + 2)
                for i in range(2):
                    t, out = 2 * half + i, PS[:, 6 * BANK + i * H:6 * BANK + (i + 1) * H]
                    for h in range(4):
                        a, w = OT[:, h, t * P:(t + 1) * P], W[:, O0 + h * H:O0 + (h + 1) * H]
                        if layer1:
                            last = product_exact(nc, out, a.hi, w, h == 0, h == 3)
                        else:
                            last = product(nc, out, a, w, h == 0, h == 3)
                last.then_inc(L["y"], 1)

            def batch_event(li, what, batch):
                {"P": project, "T": turn, "Y": output}[what](li, *batch)

            def attention(li, g, first_group, last_group):
                L, layer1 = layers[li], li == 1
                units = 8 if layer1 else 16
                pairs = units // 2
                heads = pairs // 2

                def score(u):
                    h, b = (u // 2) % heads, u // (2 * heads)
                    t, base = 2 * b + u % 2, 2 * BANK * (u % 2)
                    tok = slice(t * P, (t + 1) * P)
                    if u % (2 * heads) == 0:
                        pe.wait_ge(L["t_lo"], g * 10 + 5 * b + 5)
                        pe.wait_ge(L["v_lo"], g * 6 + 3 * b + 3)
                    if first_group and u == 1:
                        pe.wait_ge(L["x_done"], 1)
                    if u >= 2 or not first_group:
                        pe.wait_ge(L["prob"], g * units + u - 1)
                    product(nc, PS[:, base:base + 512], QT[:, (2 + h) if layer1 else h, tok],
                            KT[:, b * 512:(b + 1) * 512], True, True)
                    own = PS[:, base + 512:base + 768]
                    last = product(nc, own, QT[:, h, tok], KT[:, NCTX + b * 256:NCTX + (b + 1) * 256],
                                   True, layer1)
                    if not layer1:
                        last = nc.tensor.matmul(own, ident_r[:, :], mask_r[:, t % 2, :], start=False, stop=True)
                    last.then_inc(L["scores"], 1)

                def turn_probs(u):
                    pe.wait_ge(L["pnorm"], g * units + u + 1)
                    if u >= 1 or not first_group:
                        pe.wait_ge(L["pt_lo"], g * units + u)
                    for k in range(6):
                        last = nc.tensor.transpose(PS[:, 4 * BANK + k * P:4 * BANK + (k + 1) * P],
                                                   prob[:, u % 2, k * P:(k + 1) * P], ident[:, :])
                    last.then_inc(L["pt"], 1)

                def weigh(p):
                    b, out = p % pairs // heads, 6 * BANK
                    pe.wait_ge(L["pt_lo"], g * units + 2 * p + 2)
                    if p == 0 and not first_group:
                        pe.wait_ge(L["x_done"], 2 * g + 1)
                    elif p != 0:
                        pe.wait_ge(L["o_clip"] if layer1 else L["o_lo"], g * pairs + p)
                    parts = ((0, range(4, 6)), (256, range(0, 4))) if layer1 else ((0, range(6)),)
                    for at, keys in parts:
                        for k in keys:
                            tile = b * 4 + k if k < 4 else CT + b * 2 + k - 4
                            last = product(nc, PS[:, out + at:out + at + 256], V[:, tile, :],
                                           PT[:, p % 2, k, :], k == keys[0], k == keys[-1])
                    last.then_inc(L["outt"], 1)

                for s in steps_of(units, last_group):
                    if s < units:
                        score(s)
                    for event in events_of(li, g, s, first_group, last_group, (0,)):
                        batch_event(li, *event)
                    if (2 <= s or not first_group) and s < units + 2:
                        turn_probs(s - 2)
                    for event in events_of(li, g, s, first_group, last_group, (1,)):
                        batch_event(li, *event)
                    if (4 <= s or not first_group) and s % 2 == 0:
                        weigh((s - 4) // 2)
                    for event in events_of(li, g, s, first_group, last_group, (2,)):
                        batch_event(li, *event)
                if last_group:
                    for half in range(2):
                        output(li, g, half)

            def route(M, r, n, N):
                pe.wait_ge(N["lo"], N["nth_split"])
                for t in range(TT):
                    for c in range(HC):
                        last = product(nc, PS[:, 6 * BANK + t * n:6 * BANK + (t + 1) * n],
                                       xT[:, c, t * P:(t + 1) * P], r[:, c, :], c == 0, c == HC - 1)
                last.then_inc(M["logits"], 1)

            pe.wait_ge(ident_loaded, 16)
            turn_rows(norms[0])
            pe.wait_ge(norms[0]["lo"], 1)
            for what, k in FIRST_ORDER:
                if (what, k) == ("P", 3):
                    pe.wait_ge(ctx_lo, 1)
                batch_event(0, what, (0, 0, k))
            pe.wait_ge(consts, N_CONSTS)
            each_group(nc.tensor, 4, lambda g, first, last: attention(0, g, first, last))

            if stages >= 2:
                M = moes[0]
                turn_rows(norms[1])
                route(M, r0, E0, norms[1])

                def experts0(i, last_pair):
                    for j in range(2):
                        e = 2 * i + j
                        up = W[:, j * EW:j * EW + EUP].view("p (c n) -> p c n", c=HC)
                        down = W[:, j * EW + EUP:(j + 1) * EW].view("p (m n) -> p m n", m=4)
                        pe.wait_ge(M["w_lo"], e + 1)
                        for m in range(4):
                            for c in range(HC):
                                last = product(nc, bank(m), up[:, c, m * P:(m + 1) * P], xT[:, c, :],
                                               c == 0, c == HC - 1)
                            last.then_inc(M["up"], 1)
                        pe.wait_ge(M["x_done"], e + 1)
                        for m in range(4):
                            pe.wait_ge(M["a_lo"], 4 * e + m + 1)
                            for t in range(TT):
                                last = product(nc, bank(4 + t, H), QT[:, m, t * P:(t + 1) * P], down[:, m, :],
                                               m == 0, m == 3)
                        last.then_inc(M["y"], 1)
                each(nc.tensor, E0 // 2, experts0)

            if stages >= 3:
                turn_rows(norms[3])
                pe.wait_ge(norms[3]["q_dve"], 2)
                pe.wait_ge(norms[3]["q"], 2)
                for what, k in FIRST_ORDER:
                    batch_event(1, what, (0, 0, k))
                each_group(nc.tensor, 8, lambda g, first, last: attention(1, g, first, last))

            if stages >= 4:
                M = moes[1]
                turn_rows(norms[4])
                route(M, r1, NE1, norms[4])
                for k, src in ((0, RT[3]), (1, RT[2])):
                    pe.wait_ge(M["gates"], k + 1)
                    for t in range(TT):
                        last = nc.tensor.transpose(PS[0:NE1, 7 * BANK + t * P:7 * BANK + (t + 1) * P],
                                                   src[:, t * NE1:(t + 1) * NE1], ident[:, :])
                    last.then_inc(M["turned"], 1)
                    if k == 0:
                        pe.wait_ge(M["route_exp"], 2)
                        for t in range(TT):
                            last = nc.tensor.matmul(PS[:, 6 * BANK + t * NE1:6 * BANK + (t + 1) * NE1],
                                                    hf[0:NE1, 3, t * P:(t + 1) * P], perm[:, :],
                                                    start=True, stop=True)
                        last.then_inc(M["flat"], 1)

                def mask_up(j):
                    for c in range(HC):
                        mu = W[0:NE1, j * EW + G_MU + c * P:j * EW + G_MU + (c + 1) * P]
                        last = product(nc, bank(6 + c), mu, softT[:, :], True, True)
                    last.then_inc(M["xg"], 1)

                pe.wait_ge(M["x_done"], 1)
                pe.wait_ge(M["w_lo"], 1)
                mask_up(0)

                def experts1(i, last_pair):
                    for j in range(2):
                        e = 2 * i + j
                        w0 = j * EW
                        xg = ctxT[:, j, :].view("p (c n) -> p c n", c=HC)
                        pe.wait_ge(M["xg_lo"], e + 1)
                        for k in range(2):
                            for which in range(2):
                                for c in range(HC):
                                    at = w0 + (G_GATE, G_UP)[which] + c * I1 + k * IH
                                    last = product(nc, bank(2 * k + which, rows=IH), W[:, at:at + IH],
                                                   xg[:, c, :], c == 0, c == HC - 1)
                            last.then_inc(M["up"], 1)
                        if not (last_pair and j == 1):
                            pe.wait_ge(M["w_lo"], e + 2)
                            mask_up(1 - j)
                        pe.wait_ge(M["a_lo"], 2 * e + 2)
                        pe.wait_ge(M["x_done"], e + 1)
                        for t in range(TT):
                            for k in range(2):
                                at = w0 + G_DN + k * H
                                last = product(nc, PS[:, 4 * BANK + t * H:4 * BANK + (t + 1) * H],
                                               QT[0:IH, k, t * P:(t + 1) * P], W[0:IH, at:at + H], k == 0, k == 1)
                        last.then_inc(M["y"], 1)
                each(nc.tensor, G1 // 2, experts1)

        @blk.scalar
        def _(act):
            rows45 = PS[:, 4 * BANK:6 * BANK].rearrange("p (c n) -> p c n", c=HC)

            def split_rows(N):
                act.wait_ge(N["turned"], N["nth_turn"])
                nc.scalar.activation(xT.hi[:, :, :], rows45, ACT.Copy).then_inc(N["hi"], 1)

            def batch_event(li, what, batch):
                if what == "Y":
                    return
                g, b, k = batch
                L, layer1 = layers[li], li == 1
                n = g * 10 + 5 * b + k
                if what == "P":
                    raw = KN[:, 1, n_par(b, k) * 512:(n_par(b, k) + 1) * 512]
                    act.wait_ge(L["proj"], n + 1)
                    if not first_of_all(g, b) or k == 4:
                        act.wait_ge(L["v_lo"], g * 6 + 3 * b + (-1, 0, 0, 0, 1)[k])
                    if first_of_all(g, b) and k >= 2:
                        act.wait_ge(L["norm"], k - 1)
                    nc.scalar.activation(raw, bank(p_bank(g, b, k)), ACT.Copy).then_inc(L["raw"], 1)
                    if not layer1:
                        width = P if k < 2 else 256
                        blocks = 512 // width
                        act.wait_ge(L["raw"], n + 1)
                        if not first_of_all(g, b) or k >= 1:
                            act.wait_ge(L["sums"], n)
                        nc.scalar.activation(SQB[:, 0:blocks * P].rearrange("p (n d) -> p n d", d=P),
                                             raw.rearrange("p (n d) -> p n d", d=width)[:, :, 0:P],
                                             ACT.Square).then_inc(L["squares"], 1)
                    return
                act.wait_ge(L["turned"], n + 1)
                if not first_of_all(g, b) or k >= 2:
                    act.wait_ge(L["t_lo"], n - 1)
                width = 512 if k < 2 else 256
                tv = TV[:, 0, n_par(b, k) * 512:n_par(b, k) * 512 + width]
                if layer1 and k < 2:
                    for m in range(2):
                        last = nc.scalar.activation(tv[:, m * 256:(m + 1) * 256],
                                                    bank(t_bank(g, b, k))[:, m * 256:(m + 1) * 256], ACT.Identity,
                                                    bias=q_ln[:, 2 * m + 1:2 * m + 2], scale=q_ln[:, 2 * m:2 * m + 1])
                elif layer1:
                    v = V_KLN if k == 2 else V_KXLN
                    last = nc.scalar.activation(tv, bank(t_bank(g, b, k), width), ACT.Identity,
                                                bias=vec[:, v + 1:v + 2], scale=vec[:, v:v + 1])
                elif k >= 3:
                    last = nc.scalar.activation(tv, bank(t_bank(g, b, k), width), ACT.Copy, scale=vec[:, V_KNORM:V_KNORM + 1])
                else:
                    last = nc.scalar.activation(tv, bank(t_bank(g, b, k), width), ACT.Copy)
                last.then_inc(L["t_vec"], 1)

            def scale_part(L, k, part):
                a, half = ((Q0, 256), (KV0, 128))[part]
                if part == 0:
                    act.wait_ge(L["w_in"], 32 * k + 32)
                else:
                    act.wait_ge(L["kv_in"], 16 * k + 16)
                for c in range(HC):
                    for j in range(2):
                        at, col = a + (2 * c + j) * half, 2 * (2 * part + j) + c
                        last = nc.scalar.activation(W_raw[:, at:at + half], W_raw[:, at:at + half], ACT.Copy,
                                                    scale=in_ws[:, col:col + 1])
                last.then_inc(L["w_scaled"], 1)

            def attention(li, g, first_group, last_group):
                L, layer1 = layers[li], li == 1
                units = 8 if layer1 else 16
                pairs = units // 2
                heads = pairs // 2

                for s in steps_of(units, last_group):
                    for event in events_of(li, g, s, first_group, last_group, (0,)):
                        batch_event(li, *event)
                    for part in range(2):
                        if layer1 and not last_group and s == (SPLITS[1][0] - 1, SPLITS[1][1])[part]:
                            scale_part(L, g + 1, part)
                    if (2 <= s or not first_group) and s < units + 2:
                        u = s - 2
                        act.wait_ge(L["pt"], g * units + u + 1)
                        nc.scalar.activation(PT.hi[:, (u // 2) % 2, :, (u % 2) * P:(u % 2 + 1) * P],
                                             PS[:, 4 * BANK:4 * BANK + 768].rearrange("p (k n) -> p k n", k=6),
                                             ACT.Copy).then_inc(L["pt_hi"], 1)
                    if not layer1 and (1 <= s or not first_group) and s <= units:
                        u = s - 1
                        act.wait_ge(L["rsum"], g * units + u + 1)
                        nc.scalar.activation(prob[:, u % 2, :], prob[:, u % 2, :], ACT.Copy,
                                             scale=RC[:, u % 4, 0:1]).then_inc(L["pnorm"], 1)
                    if s < units:
                        base = 2 * BANK * (s % 2)
                        act.wait_ge(L["nmax"], g * units + s + 1)
                        if layer1:
                            nc.scalar.activation(prob[:, s % 2, 0:512], PS[:, base:base + 512], ACT.Exp,
                                                 bias=NM[:, s % 4, 0:1],
                                                 accum_out=SM[:, s % 4, 0:1])
                            last = nc.scalar.activation(prob[:, s % 2, 512:768], PS[:, base + 512:base + 768],
                                                        ACT.Exp, bias=NM[:, s % 4, 1:2],
                                                        accum_out=SM[:, s % 4, 1:2])
                        else:
                            col = (2 * (s // (2 * heads)) + s % 2) * 4 + (s // 2) % heads
                            last = nc.scalar.activation(prob[:, s % 2, :], PS[:, base:base + 768], ACT.Exp,
                                                        bias=NM[:, s % 4, 0:1], scale=RQ[:, col:col + 1],
                                                        accum_out=SM[:, s % 4, 0:1])
                        last.then_inc(L["prob"], 1)
                    for event in events_of(li, g, s, first_group, last_group, (1, 2)):
                        batch_event(li, *event)
                    if layer1 and (1 <= s or not first_group) and s <= units:
                        u = s - 1
                        act.wait_ge(L["rsum"], g * units + u + 1)
                        for k, (a, z) in enumerate(((0, 512), (512, 768))):
                            last = nc.scalar.activation(prob[:, u % 2, a:z], prob[:, u % 2, a:z], ACT.Copy,
                                                        scale=RC[:, u % 4, k:k + 1])
                        last.then_inc(L["pnorm"], 1)
                    if not layer1 and (s >= 4 or not first_group) and s % 2 == 0:
                        p = (s - 4) // 2
                        b = p % pairs // heads
                        act.wait_ge(L["outt"], g * pairs + p + 1)
                        nc.scalar.activation(OT.hi[:, p % heads, b * 256:(b + 1) * 256], bank(6, 256),
                                             ACT.Copy).then_inc(L["o_hi"], 1)

            split_rows(norms[0])
            act.wait_ge(ctx_loaded, 16)
            nc.scalar.activation(ctxT.hi[:, :, :], ctx_raw[:, :, :], ACT.Copy).then_inc(ctx_hi, 1)
            act.wait_ge(vec_loaded, 16)
            for what, k in FIRST_ORDER:
                batch_event(0, what, (0, 0, k))
            each_group(nc.scalar, 4, lambda g, first, last: attention(0, g, first, last))

            if stages >= 2:
                M = moes[0]
                split_rows(norms[1])
                act.wait_ge(M["gates"], 1)
                nc.scalar.activation(RS[:, 6, 0:4], RS[:, 5, 0:4], ACT.Exp).then_inc(M["route_exp"], 1)

                def experts0(i, last_pair):
                    for j in range(2):
                        e = 2 * i + j
                        for m in range(4):
                            act.wait_ge(M["up"], 4 * e + m + 1)
                            nc.scalar.activation(hf[:, m, :], bank(m), ACT.Silu).then_inc(M["act"], 1)
                each(nc.scalar, E0 // 2, experts0)

            if stages >= 3:
                for part in range(2):
                    scale_part(layers[1], 0, part)
                N = norms[3]
                act.wait_ge(N["turned"], N["nth_turn"])
                for c in range(HC):
                    last = nc.scalar.activation(TV[:, 0, c * T:(c + 1) * T], rows45[:, c, :], ACT.Identity,
                                                bias=vec[:, V_LN + 2 + c:V_LN + 3 + c],
                                                scale=vec[:, V_LN + c:V_LN + c + 1])
                last.then_inc(N["vec"], 1)
                act.wait_ge(N["vec"], 1)
                for j in range(4):
                    if j >= 2:
                        act.wait_ge(N["bf"], j - 1)
                    for c in range(HC):
                        last = nc.scalar.activation(q_in[j % 2][:, c * T:(c + 1) * T], TV[:, 0, c * T:(c + 1) * T],
                                                    ACT.Copy, scale=in_rcp[:, 2 * j + c:2 * j + c + 1])
                    last.then_inc(N["scaled"], 1)
                for what, k in FIRST_ORDER:
                    batch_event(1, what, (0, 0, k))
                each_group(nc.scalar, 8, lambda g, first, last: attention(1, g, first, last))

            if stages >= 4:
                M, N = moes[1], norms[4]
                split_rows(N)
                nc.scalar.activation(hf[:, 0:2, :], rows45, ACT.Copy).then_inc(N["vec"], 1)
                act.wait_ge(M["route"], 2)
                nc.scalar.activation(RT[1][:, :], RT[0][:, :], ACT.Exp).then_inc(M["route_exp"], 1)
                act.wait_ge(M["turned"], 1)
                nc.scalar.activation(hf[0:NE1, 3, :], bank(7, rows=NE1), ACT.Copy).then_inc(M["route_exp"], 1)
                act.wait_ge(M["xg_sum"], 1)
                nc.scalar.activation(RT[1][:, :], RT[0][:, :], ACT.Exp).then_inc(M["route_exp"], 1)
                act.wait_ge(M["turned"], 2)
                nc.scalar.activation(softT.hi[:, :], bank(7, rows=NE1), ACT.Copy).then_inc(M["route_exp"], 1)

                def experts1(i, last_pair):
                    for j in range(2):
                        e = 2 * i + j
                        for k in range(2):
                            act.wait_ge(M["up"], 2 * e + k + 1)
                            nc.scalar.activation(KN[0:IH, 0, k * T:(k + 1) * T], bank(2 * k, rows=IH), ACT.Silu)\
                              .then_inc(M["act"], 1)
                each(nc.scalar, G1 // 2, experts1)

        @blk.vector
        def _(dve):
            rows45 = PS[:, 4 * BANK:6 * BANK].rearrange("p (c n) -> p c n", c=HC)

            def norm_rows(N, src, dst, ready):
                if ready:
                    dve.wait_ge(*ready)
                for t in range(TT):
                    last = nc.vector.bn_stats(stat[:, t, :], src[:, t, :])
                last.then_inc(N["sums"], 1)
                dve.wait_ge(N["sums"], N["nth"])
                for t in range(TT):
                    last = nc.vector.bn_aggr(mv[:, 0, t, :], stat[:, t, :])
                last.then_inc(N["aggr"], 1)
                dve.wait_ge(N["rstd"], N["nth"])
                for t in range(TT):
                    last = nc.vector.tensor_scalar(dst[:, t, :], src[:, t, :], mv[:, 0, t, 0:1], rr[:, 0, t:t + 1],
                                                   ALU.subtract, ALU.mult)
                last.then_inc(N["norm"], 1)

            def split_rows(N):
                dve.wait_ge(N["hi"], N["nth_split"])
                if N["nth_vec"]:
                    dve.wait_ge(N["vec"], N["nth_vec"])
                nc.vector.tensor_tensor(xT.lo[:, :, :], rows45, f32(xT.hi[:, :, :]), ALU.subtract)\
                  .then_inc(N["lo"], 1)

            def split_part(L, layer1, k, part):
                a, z = ((Q0, O0), (KV0, Q0), (CKV0, KV0))[part]
                if L is layers[0] and isinstance(k, int) and k == 0 and part == 0:
                    dve.wait_ge(first_q_in, 16)
                elif layer1 and part == 0:
                    dve.wait_ge(L["w_scaled"], 2 * k + 1)
                else:
                    dve.wait_ge(L["w_in"], (32 if layer1 else 16) * (k + 1))
                nc.vector.tensor_copy(W.hi[:, a:z], W_raw[:, a:z]).then_inc(L["w_hi"], 1)

            def t_hi(li, g, b, k):
                L, n = layers[li], g * 10 + 5 * b + k
                dve.wait_ge(L["t_vec"], n + 1)
                if k >= 2:
                    at = NCTX + b * 256 if k == 2 else b * 512 + (k - 3) * 256
                    ins = nc.vector.tensor_copy(KT.hi[:, at:at + 256],
                                                TV[:, 0, n_par(b, k) * 512:n_par(b, k) * 512 + 256])
                else:
                    t = 2 * b + k
                    tv = TV[:, 0, n_par(b, k) * 512:(n_par(b, k) + 1) * 512]
                    ins = nc.vector.tensor_copy(QT.hi[:, :, t * P:(t + 1) * P],
                                                tv.rearrange("p (h n) -> p h n", h=4))
                ins.then_inc(L["t_hi"], 1)

            def front(li, g, b, k):
                L, layer1 = layers[li], li == 1
                n, par = g * 10 + 5 * b + k, n_par(b, k)
                width = P if k < 2 else 256
                blocks = 512 // width
                raw = KN[:, 1, par * 512:(par + 1) * 512].rearrange("p (n d) -> p n d", d=width)
                if layer1:
                    if not first_of_all(g, b) or k >= 1:
                        dve.wait_ge(L["aggr"], n)
                    dve.wait_ge(L["raw"], n + 1)
                    for m in range(blocks):
                        last = nc.vector.bn_stats(stat[:, m, :], raw[:, m, 0:P])
                    last.then_inc(L["sums"], 1)
                    dve.wait_ge(L["sums"], n + 1)
                    if k < 2:
                        nc.vector.tensor_copy(tick[:, :], stat[:, 0, 0:1])
                else:
                    if not first_of_all(g, b) or k >= 2:
                        dve.wait_ge(L["var"], n - 1)
                    dve.wait_ge(L["squares"], n + 1)
                    nc.vector.tensor_reduce(ssum[:, par, 0:blocks],
                                            SQB[:, 0:blocks * P].rearrange("p (n d) -> p n d", d=P),
                                            AX.X, ALU.add).then_inc(L["sums"], 1)
                if k >= 2:
                    v0 = CT + 2 * b if k == 2 else b * 4 + 2 * k - 6
                    nc.vector.tensor_copy(V.hi[:, v0:v0 + 2, :], raw[:, :, P:256]).then_inc(L["v_hi"], 1)
                if layer1:
                    for m in range(blocks):
                        last = nc.vector.bn_aggr(mv[:, par, m, :], stat[:, m, :])
                    last.then_inc(L["aggr"], 1)

            def back(li, g, b, k):
                L, layer1 = layers[li], li == 1
                n, par = g * 10 + 5 * b + k, n_par(b, k)
                width = P if k < 2 else 256
                blocks = 512 // width
                raw = KN[:, 1, par * 512:(par + 1) * 512].rearrange("p (n d) -> p n d", d=width)
                kn = KN[:, 0, par * 512:par * 512 + blocks * P].rearrange("p (n d) -> p n d", d=P)
                if layer1:
                    dve.wait_ge(L["rstd"], n + 1)
                    for m in range(blocks):
                        last = nc.vector.tensor_scalar(kn[:, m, :], raw[:, m, 0:P], mv[:, par, m, 0:1],
                                                       rr[:, par, m:m + 1], ALU.subtract, ALU.mult)
                    last.then_inc(L["norm"], 1)
                    return
                scale = rr[:, par, 0:blocks].rearrange("p (n o) -> p n o", o=1).broadcast_to([P, blocks, P])
                if k >= 3:
                    dve.wait_ge(L["rstd"], n + 1)
                    nc.vector.scalar_tensor_tensor(kn, raw[:, :, 0:P], ROOT_D, scale, ALU.mult, ALU.mult)\
                      .then_inc(L["norm"], 1)
                    return
                def table(part, a, z):
                    if k == 2:
                        return rope_w[:, 1, part, :, a:z]
                    return rope_w[:, 0, part, k:k + 1, a:z].broadcast_to([P, 4, z - a])
                rp = RP[:, 0:blocks * P].rearrange("p (n d) -> p n d", d=P)
                if not first_of_all(g, b) or k >= 1:
                    dve.wait_ge(L["norm"], n)
                nc.vector.tensor_tensor(rp, raw[:, :, 0:P], table(0, 0, P), ALU.mult)
                nc.vector.tensor_tensor(kn[:, :, 0:64], raw[:, :, 64:P], table(1, 0, 64), ALU.mult)
                nc.vector.tensor_tensor(kn[:, :, 64:P], raw[:, :, 0:64], table(1, 64, P), ALU.mult)\
                  .then_inc(L["roped"], 1)
                dve.wait_ge(L["roped"], g * 6 + 3 * b + k + 1)
                if k == 2:
                    nc.vector.tensor_tensor(kn, kn, rp, ALU.add).then_inc(L["rope_sum"], 1)
                    dve.wait_ge(L["rope_sum"], g * 2 + b + 1)
                    dve.wait_ge(L["rstd"], n + 1)
                    nc.vector.scalar_tensor_tensor(kn, kn, ROOT_D, scale, ALU.mult, ALU.mult)\
                      .then_inc(L["norm"], 1)
                else:
                    nc.vector.tensor_tensor(kn, kn, rp, ALU.add).then_inc(L["norm"], 1)

            def first_batches(li):
                for what, k in FIRST_ORDER:
                    if what == "P":
                        front(li, 0, 0, k)
                    else:
                        t_hi(li, 0, 0, k)
                    if what == "P" and k >= 1 or k == 3:
                        back(li, 0, 0, k - 1 if what == "P" else 4)

            def add_output(li, g, half):
                L = layers[li]
                dve.wait_ge(L["y"], 2 * g + half + 1)
                x = X[:, 2 * half:2 * half + 2, :]
                y = bank(6).rearrange("p (t n) -> p t n", t=2)
                if li == 1:
                    last = nc.vector.scalar_tensor_tensor(x, y, out_ws[:, 0:1], x, ALU.mult, ALU.add)
                else:
                    last = nc.vector.tensor_tensor(x, y, x, ALU.add)
                last.then_inc(L["x_done"], 1)

            def attention(li, g, first_group, last_group):
                L, layer1 = layers[li], li == 1
                units = 8 if layer1 else 16
                pairs = units // 2
                heads = pairs // 2

                def take_reciprocals(s):
                    if (1 <= s or not first_group) and s <= units:
                        q, n = (s - 1) % 4, 2 if layer1 else 1
                        dve.wait_ge(L["prob"], g * units + s)
                        nc.vector.reciprocal(RC[:, q, 0:n], SM[:, q, 0:n]).then_inc(L["rsum"], 1)

                waiting = []
                for s in steps_of(units, last_group):
                    if not layer1:
                        take_reciprocals(s)
                    if s < units:
                        base, q = 2 * BANK * (s % 2), s % 4
                        dve.wait_ge(L["scores"], g * units + s + 1)
                        if layer1:
                            nc.vector.tensor_reduce(NM[:, q, 0:1], PS[:, base:base + 512], AX.X, ALU.max, negate=True)
                            nc.vector.tensor_reduce(NM[:, q, 1:2], PS[:, base + 512:base + 768], AX.X, ALU.max,
                                                    negate=True).then_inc(L["nmax"], 1)
                        else:
                            col = (2 * (s // (2 * heads)) + s % 2) * 4 + (s // 2) % heads
                            nc.vector.tensor_reduce(MX[:, q, 0:1], PS[:, base:base + 768], AX.X, ALU.max)\
                              .then_inc(L["rowmax"], 1)
                            dve.wait_ge(L["rowmax"], g * units + s + 1)
                            nc.vector.scalar_tensor_tensor(NM[:, q, 0:1], MX[:, q, 0:1], -1.0, RQ[:, col:col + 1],
                                                           ALU.mult, ALU.mult).then_inc(L["nmax"], 1)
                    if layer1:
                        take_reciprocals(s)
                    for due in waiting:
                        back(li, *due)
                    waiting = []
                    if (2 <= s or not first_group) and s < units + 2:
                        u = s - 2
                        cols = slice((u % 2) * P, (u % 2 + 1) * P)
                        dve.wait_ge(L["pt_hi"], g * units + u + 1)
                        nc.vector.tensor_tensor(PT.lo[:, (u // 2) % 2, :, cols],
                                                PS[:, 4 * BANK:4 * BANK + 768].rearrange("p (k n) -> p k n", k=6),
                                                f32(PT.hi[:, (u // 2) % 2, :, cols]), ALU.subtract)\
                          .then_inc(L["pt_lo"], 1)
                    if layer1 and s == 3:
                        dve.wait_ge(L["wo_in"], 16 * g + 16)
                        nc.vector.reciprocal(srs[:, :], W_raw[:, SM0:GW]).then_inc(L["smooth"], 1)
                    if (s >= 4 or not first_group) and s % 2 == 0:
                        p = (s - 4) // 2
                        h, b, n = p % heads, p % pairs // heads, g * pairs + p + 1
                        if not layer1:
                            cols = slice(b * 256, (b + 1) * 256)
                            dve.wait_ge(L["o_hi"], n)
                            nc.vector.tensor_tensor(OT.lo[:, h, cols], bank(6, 256), f32(OT.hi[:, h, cols]),
                                                    ALU.subtract).then_inc(L["o_lo"], 1)
                        else:
                            dve.wait_ge(L["outt"], n)
                            for k in range(2):
                                last = nc.vector.tensor_scalar(SQ[:, k * 256:(k + 1) * 256],
                                                               PS[:, 6 * BANK + k * 256:6 * BANK + (k + 1) * 256],
                                                               srs[:, 2 * k + h:2 * k + h + 1], FP8_MAX,
                                                               ALU.mult, ALU.min)
                            last.then_inc(L["o_clip"], 1)
                            dve.wait_ge(L["o_clip"], n)
                            if p == 0 and first_group:
                                dve.wait_ge(L["smooth"], 1)
                            else:
                                dve.wait_ge(L["o_q"], n - 1)
                            nc.vector.tensor_scalar(QY[:, 0:T], SQ[:, 0:T], -FP8_MAX, None, ALU.max)\
                              .then_inc(L["o_bf"], 1)
                            dve.wait_ge(L["o_bf"], n)
                            nc.vector.tensor_scalar(QE[:, 0:T].bitcast(U16), QY[:, 0:T].bitcast(U16), 0x7F80, None,
                                                    ALU.bitwise_and).then_inc(L["o_exp"], 1)
                            dve.wait_ge(L["o_exp"], n)
                            nc.vector.tensor_scalar(RP[:, 512:1024], QE[:, 0:T], FP8_MIN_NORMAL, FP8_MAGIC,
                                                    ALU.max, ALU.mult).then_inc(L["o_magic"], 1)
                    for what, batch in events_of(li, g, s, first_group, last_group):
                        if what == "P":
                            front(li, *batch)
                            waiting.append(batch)
                        elif what == "T":
                            for due in waiting:
                                if due[2] == batch[2]:
                                    back(li, *due)
                            waiting = [due for due in waiting if due[2] != batch[2]]
                            t_hi(li, *batch)
                        else:
                            for due in waiting:
                                back(li, *due)
                            waiting = []
                            add_output(li, *batch)
                    for part in (0, 2) if layer1 else (0, 1, 2):
                        if s == SPLITS[li][part] and not last_group:
                            split_part(L, layer1, g + 1, part)
                    if s == SPLITS[li][3]:
                        dve.wait_ge(L["wo_in"], 16 * g + 16)
                        nc.vector.tensor_copy(W.hi[:, O0:SM0], W_raw[:, O0:SM0]).then_inc(L["wo_hi"], 1)
                if last_group:
                    for half in range(2):
                        add_output(li, g, half)

            dve.wait_ge(x_loaded, 16)
            norm_rows(norms[0], X, XN, None)
            split_part(layers[0], False, 0, 0)
            split_rows(norms[0])
            for part in (1, 2):
                split_part(layers[0], False, 0, part)
            dve.wait_ge(loaded, 16 * LOADS)
            nc.vector.tensor_copy(ident_r[:, :], ident[:, :]).then_inc(consts, 1)
            nc.vector.tensor_copy(mask_r[:, :, :], mask[:, :, :]).then_inc(consts, 1)
            for j in range(2):
                row = rows[:, j:j + 1, :]
                nc.vector.tensor_tensor(rope_w[:, j, 0, :, :], rope[:, 0, :, :], row.broadcast_to([P, 2, P]),
                                        ALU.mult).then_inc(consts, 1)
                nc.vector.tensor_tensor(rope_w[:, j, 1, :, 0:64], rope[:, 1, :, 0:64],
                                        row[:, :, 64:P].broadcast_to([P, 2, 64]), ALU.mult).then_inc(consts, 1)
                nc.vector.tensor_tensor(rope_w[:, j, 1, :, 64:P], rope[:, 1, :, 64:P],
                                        row[:, :, 0:64].broadcast_to([P, 2, 64]), ALU.mult).then_inc(consts, 1)
            nc.vector.tensor_scalar(q_ln[:, 0:2], vec[:, V_QLN:V_QLN + 2], HEAD_SCALE, None, ALU.mult).then_inc(consts, 1)
            nc.vector.tensor_scalar(q_ln[:, 2:4], vec[:, V_QXLN:V_QXLN + 2], HEAD_SCALE, None, ALU.mult)\
              .then_inc(consts, 1)
            nc.vector.reciprocal(in_rcp[:, :], vec[:, V_IN:V_IN + 8]).then_inc(consts, 1)
            for j in range(4):
                last = nc.vector.tensor_scalar(in_ws[:, 2 * j:2 * j + 2], vec[:, V_IN + 2 * j:V_IN + 2 * j + 2],
                                               vec[:, V_WS + j:V_WS + j + 1], None, ALU.mult)
            last.then_inc(consts, 1)
            nc.vector.tensor_copy(r0.hi[:, :, :], r0_raw[:, :, :]).then_inc(consts, 1)
            nc.vector.tensor_copy(r1.hi[:, :, :], r1_raw[:, :, :]).then_inc(consts, 1)
            dve.wait_ge(consts, N_CONSTS - 2)
            nc.vector.tensor_tensor(r0.lo[:, :, :], r0_raw[:, :, :], f32(r0.hi[:, :, :]), ALU.subtract)\
              .then_inc(consts, 1)
            nc.vector.tensor_tensor(r1.lo[:, :, :], r1_raw[:, :, :], f32(r1.hi[:, :, :]), ALU.subtract)\
              .then_inc(consts, 1)
            nc.vector.tensor_scalar(perm[:, :], inv[:, :], vec[0:NE1, V_PIDX:V_PIDX + 1], None, ALU.is_equal)\
              .then_inc(layers[0]["x_done"], 1)
            first_batches(0)
            each_group(nc.vector, 4, lambda g, first, last: attention(0, g, first, last))

            def split_expert(M, e, j, width, arrived):
                dve.wait_ge((M["w_in0"], M["w_in1"])[j], arrived)
                nc.vector.tensor_copy(W.hi[:, j * EW:j * EW + width], W_raw[:, j * EW:j * EW + width])\
                  .then_inc(M["w_hi"], 1)

            def add_expert(M, e, gates, wide):
                dve.wait_ge(M["y"], e + 1)
                for t in range(TT):
                    src = bank(4 + t, H) if wide else PS[:, 4 * BANK + t * H:4 * BANK + (t + 1) * H]
                    last = nc.vector.scalar_tensor_tensor(X[:, t, :], src, gates[:, t, bass.ds(e, 1)], X[:, t, :],
                                                          ALU.mult, ALU.add)
                last.then_inc(M["x_done"], 1)

            if stages >= 2:
                M, N = moes[0], norms[1]
                norm_rows(N, X, XN, x_ready[1])
                split_rows(N)
                split_expert(M, 0, 0, EW, 16)

                steps = [0]

                def step(ins):
                    steps[0] += 1
                    ins.then_inc(M["route"], 1)
                    dve.wait_ge(M["route"], steps[0])

                def v8(k):
                    return RT[k][:, 0:TT * E0].rearrange("p (t e) -> p t e", t=TT)

                def wide(a):
                    return a.rearrange("p (t o) -> p t o", o=1).broadcast_to([P, TT, E0])

                def pick(logits, top, chosen):
                    eq, rank = v8(3), RS[:, 4, 0:4]
                    step(nc.vector.tensor_reduce(top, logits, AX.X, ALU.max))
                    step(nc.vector.tensor_tensor(eq, logits, wide(top), ALU.is_equal))
                    falling = RS[:, 7, 0:8].rearrange("p (o e) -> p o e", o=1).broadcast_to([P, TT, E0])
                    step(nc.vector.tensor_tensor(chosen, eq, falling, ALU.mult))
                    step(nc.vector.tensor_reduce(rank, chosen, AX.X, ALU.max))
                    step(nc.vector.tensor_tensor(eq, chosen, wide(rank), ALU.is_equal))
                    step(nc.vector.tensor_copy(chosen, eq))

                dve.wait_ge(M["logits"], 1)
                step(nc.vector.tensor_copy(v8(0), bank(6, TT * E0).rearrange("p (t e) -> p t e", t=TT)))
                pick(v8(0), RS[:, 0, 0:4], v8(1))
                step(nc.vector.scalar_tensor_tensor(v8(0), v8(1), -3.0e38, v8(0), ALU.mult, ALU.add))
                pick(v8(0), RS[:, 1, 0:4], v8(2))
                nc.vector.tensor_tensor(RS[:, 5, 0:4], RS[:, 1, 0:4], RS[:, 0, 0:4], ALU.subtract)\
                  .then_inc(M["gates"], 1)
                dve.wait_ge(M["route_exp"], 1)
                step(nc.vector.tensor_scalar_add(RS[:, 2, 0:4], RS[:, 6, 0:4], 1.0))
                step(nc.vector.reciprocal(RS[:, 3, 0:4], RS[:, 2, 0:4]))
                step(nc.vector.tensor_tensor(RS[:, 2, 0:4], RS[:, 6, 0:4], RS[:, 3, 0:4], ALU.mult))
                step(nc.vector.tensor_tensor(v8(1), v8(1), wide(RS[:, 3, 0:4]), ALU.mult))
                step(nc.vector.tensor_tensor(v8(2), v8(2), wide(RS[:, 2, 0:4]), ALU.mult))
                nc.vector.tensor_tensor(gate0[:, :, :], v8(1), v8(2), ALU.add).then_inc(M["x_done"], 1)
                dve.wait_ge(M["x_done"], 1)

                def experts0(i, last_pair):
                    for j in range(2):
                        e = 2 * i + j
                        for m in range(4):
                            dve.wait_ge(M["act"], 4 * e + m + 1)
                            nc.vector.tensor_copy(QT.hi[:, m, :], hf[:, m, :]).then_inc(M["a_hi"], 1)
                            dve.wait_ge(M["a_hi"], 4 * e + m + 1)
                            nc.vector.tensor_tensor(QT.lo[:, m, :], hf[:, m, :], f32(QT.hi[:, m, :]), ALU.subtract)\
                              .then_inc(M["a_lo"], 1)
                            if m == 0 and not (last_pair and j == 1):
                                split_expert(M, e + 1, 1 - j, EW, 16 * i + 16 + 16 * j)
                        add_expert(M, e, gate0, True)
                each(nc.vector, E0 // 2, experts0)

            def quantise(N):
                for j in range(4):
                    i = j % 2
                    if j >= 2:
                        dve.wait_ge(N["q" if i == 0 else "q_dve"], 1)
                    dve.wait_ge(N["scaled"], j + 1)
                    nc.vector.tensor_scalar(q_bf[i], q_in[i], FP8_MAX, -FP8_MAX, ALU.min, ALU.max)\
                      .then_inc(N["bf"], 1)
                    dve.wait_ge(N["bf"], j + 1)
                    if j >= 1:
                        dve.wait_ge(N["magic"], j)
                    nc.vector.tensor_scalar(QE[:, :].bitcast(U16), q_bf[i].bitcast(U16), 0x7F80, None,
                                            ALU.bitwise_and).then_inc(N["exp"], 1)
                    dve.wait_ge(N["exp"], j + 1)
                    nc.vector.tensor_scalar(q_magic[i], QE[:, :], FP8_MIN_NORMAL, FP8_MAGIC, ALU.max, ALU.mult)\
                      .then_inc(N["magic"], 1)
                    if i == 1:
                        dve.wait_ge(N["magic"], j + 1)
                        nc.vector.tensor_tensor(q_sum[i], q_magic[i], q_bf[i], ALU.add).then_inc(N["add_dve"], 1)
                        dve.wait_ge(N["add_dve"], j // 2 + 1)
                        nc.vector.tensor_tensor(xq[j], q_sum[i].rearrange("p (c n) -> p c n", c=HC),
                                                q_magic[i].rearrange("p (c n) -> p c n", c=HC),
                                                ALU.subtract).then_inc(N["q_dve"], 1)

            if stages >= 3:
                norm_rows(norms[2], X, XN, x_ready[2])
                dve.wait_ge(norms[2]["norm"], norms[2]["nth"])
                norm_rows(norms[3], XN, XN, None)
                for part in (0, 2):
                    split_part(layers[1], True, 0, part)
                quantise(norms[3])
                nc.vector.tensor_tensor(out_ws[:, :], vec[:, V_PS:V_PS + 1], vec[:, V_PS + 1:V_PS + 2], ALU.mult)\
                  .then_inc(layers[1]["x_done"], 1)
                first_batches(1)
                each_group(nc.vector, 8, lambda g, first, last: attention(1, g, first, last))

            if stages >= 4:
                M, N = moes[1], norms[4]
                norm_rows(N, X, XN, x_ready[3])
                split_rows(N)
                split_expert(M, 0, 0, FW, 16)
                sums = RS[:, 0:6, :]

                def v64(k):
                    return RT[k][:, :].rearrange("p (t e) -> p t e", t=TT)

                def v32(k):
                    return RT[k][:, :].rearrange("p (g i) -> p g i", i=GS)

                def by_token(k):
                    return sums[:, k, 0:TT].rearrange("p (t o) -> p t o", o=1).broadcast_to([P, TT, NE1])

                def by_group(k):
                    return sums[:, k, :].rearrange("p (g o) -> p g o", o=1).broadcast_to([P, TT * G1, GS])

                steps = [0]

                def step(ins):
                    steps[0] += 1
                    ins.then_inc(M["route"], 1)
                    dve.wait_ge(M["route"], steps[0])

                dve.wait_ge(M["logits"], 1)
                logits = bank(6, TT * NE1).rearrange("p (t e) -> p t e", t=TT)
                step(nc.vector.tensor_reduce(sums[:, 0, 0:TT], logits, AX.X, ALU.max))
                step(nc.vector.tensor_tensor(v64(0), logits, by_token(0), ALU.subtract))
                dve.wait_ge(M["route_exp"], 1)
                step(nc.vector.tensor_reduce(sums[:, 1, 0:TT], v64(1), AX.X, ALU.add))
                step(nc.vector.reciprocal(sums[:, 2, 0:TT], sums[:, 1, 0:TT]))
                step(nc.vector.tensor_tensor(v64(2), v64(1), by_token(2), ALU.mult))
                for t in range(TT):
                    last = nc.vector.max(top8[:, t, :], v64(2)[:, t, :])
                step(last)
                for t in range(TT):
                    last = nc.vector.match_replace(v64(0)[:, t, :], top8[:, t, :], v64(2)[:, t, :], 0.0)
                step(last)
                nc.vector.tensor_tensor(v64(3), v64(2), v64(0), ALU.subtract).then_inc(M["gates"], 1)
                dve.wait_ge(M["flat"], 1)
                step(nc.vector.tensor_copy(v64(2), logits))
                step(nc.vector.tensor_reduce(scal1[:, :, :].rearrange("p t g -> p (t g)"), v32(2), AX.X, ALU.add))
                step(nc.vector.tensor_scalar(v64(0), v64(2), 0.0, -1.0e9, ALU.is_equal, ALU.mult))
                step(nc.vector.tensor_tensor(v64(1), v64(2), v64(0), ALU.add))
                step(nc.vector.tensor_reduce(sums[:, 3, :], v32(1), AX.X, ALU.max))
                nc.vector.tensor_tensor(v32(0), v32(1), by_group(3), ALU.subtract).then_inc(M["xg_sum"], 1)
                dve.wait_ge(M["route_exp"], 3)
                step(nc.vector.tensor_reduce(sums[:, 4, :], v32(1), AX.X, ALU.add))
                step(nc.vector.reciprocal(sums[:, 5, :], sums[:, 4, :]))
                nc.vector.tensor_tensor(v32(2), v32(1), by_group(5), ALU.mult).then_inc(M["gates"], 1)
                dve.wait_ge(M["route_exp"], 4)
                nc.vector.tensor_tensor(softT.lo[:, :], bank(7, rows=NE1), f32(softT.hi[:, :]), ALU.subtract)\
                  .then_inc(M["x_done"], 1)

                def group_input(e, j):
                    xg = TV[:, j, :].rearrange("p (c n) -> p c n", c=HC)
                    dve.wait_ge(M["xg"], e + 1)
                    nc.vector.tensor_tensor(xg, PS[:, 6 * BANK:8 * BANK].rearrange("p (c n) -> p c n", c=HC),
                                            hf[:, 0:2, :], ALU.add).then_inc(M["xg_sum"], 1)
                    dve.wait_ge(M["xg_sum"], e + 2)
                    nc.vector.tensor_copy(ctxT.hi[:, j, :], TV[:, j, :]).then_inc(M["xg_hi"], 1)
                    dve.wait_ge(M["xg_hi"], e + 1)
                    nc.vector.tensor_tensor(ctxT.lo[:, j, :], TV[:, j, :], f32(ctxT.hi[:, j, :]), ALU.subtract)\
                      .then_inc(M["xg_lo"], 1)

                group_input(0, 0)

                def experts1(i, last_pair):
                    for j in range(2):
                        e = 2 * i + j
                        if not (last_pair and j == 1):
                            split_expert(M, e + 1, 1 - j, FW, 16 * i + 16 + 16 * j)
                        for k in range(2):
                            n, half = 2 * e + k + 1, slice(k * T, (k + 1) * T)
                            dve.wait_ge(M["act"], n)
                            nc.vector.tensor_tensor(KN[0:IH, 1, half], bank(2 * k + 1, rows=IH), KN[0:IH, 0, half],
                                                    ALU.mult).then_inc(M["prod"], 1)
                            dve.wait_ge(M["prod"], n)
                            nc.vector.tensor_copy(QT.hi[0:IH, k, :], KN[0:IH, 1, half]).then_inc(M["a_hi"], 1)
                            dve.wait_ge(M["a_hi"], n)
                            nc.vector.tensor_tensor(QT.lo[0:IH, k, :], KN[0:IH, 1, half],
                                                    f32(QT.hi[0:IH, k, :]), ALU.subtract).then_inc(M["a_lo"], 1)
                        if not (last_pair and j == 1):
                            group_input(e + 1, 1 - j)
                        add_expert(M, e, scal1, False)
                each(nc.vector, G1 // 2, experts1)

        @blk.gpsimd
        def _(pool):
            minus_half = vec[:, V_MH:V_MH + 1]

            def norm_rows(N):
                pool.wait_ge(N["aggr"], N["nth"])
                nc.gpsimd.tensor_scalar(ln_v[:, :], mv[:, 0, 0:TT, 1], 1.0, LN_EPS, ALU.mult, ALU.add)\
                  .then_inc(N["var"], 1)
                pool.wait_ge(N["var"], N["nth"])
                nc.gpsimd.tensor_tensor(rr[:, 0, 0:TT], ln_v[:, :], minus_half.broadcast_to([P, TT]), ALU.pow)\
                  .then_inc(N["rstd"], 1)

            def split_part(L, k, part):
                a, z = ((Q0, O0), (KV0, Q0), (CKV0, KV0))[part]
                pool.wait_ge(L["w_hi"], 3 * k + part + 1 if L is layers[0] else 2 * k + part // 2 + 1)
                nc.gpsimd.tensor_tensor(W.lo[:, a:z], W_raw[:, a:z], f32(W.hi[:, a:z]), ALU.subtract)\
                  .then_inc(L["w_lo"], 1)

            def batch_event(li, what, batch):
                if what == "Y":
                    return
                g, b, k = batch
                L, layer1 = layers[li], li == 1
                n, par = g * 10 + 5 * b + k, n_par(b, k)
                if what == "P":
                    blocks = 4 if k < 2 else 2
                    spread = mv[:, par, 0:blocks, 1] if layer1 else ssum[:, par, 0:blocks]
                    eps = vec[:, V_EPS + li:V_EPS + li + 1].broadcast_to([P, blocks])
                    pool.wait_ge(L["aggr"] if layer1 else L["sums"], n + 1)
                    nc.gpsimd.tensor_tensor(vv[:, par, 0:blocks], spread, eps, ALU.add).then_inc(L["var"], 1)
                    pool.wait_ge(L["var"], n + 1)
                    t = 2 * b + k
                    root = RQ[:, t * 4:t * 4 + 4] if not layer1 and k < 2 else rr[:, par, 0:blocks]
                    nc.gpsimd.tensor_tensor(root, vv[:, par, 0:blocks], minus_half.broadcast_to([P, blocks]),
                                            ALU.pow).then_inc(L["rstd"], 1)
                if what == "P" and k >= 2:
                    v0 = CT + 2 * b if k == 2 else b * 4 + 2 * k - 6
                    raw = KN[:, 1, par * 512:(par + 1) * 512].rearrange("p (n d) -> p n d", d=256)
                    pool.wait_ge(L["v_hi"], g * 6 + 3 * b + k - 1)
                    nc.gpsimd.tensor_tensor(V.lo[:, v0:v0 + 2, :], raw[:, :, P:256], f32(V.hi[:, v0:v0 + 2, :]),
                                            ALU.subtract).then_inc(L["v_lo"], 1)
                if what == "T":
                    pool.wait_ge(L["t_hi"], n + 1)
                    if k >= 2:
                        at = NCTX + b * 256 if k == 2 else b * 512 + (k - 3) * 256
                        ins = nc.gpsimd.tensor_tensor(KT.lo[:, at:at + 256],
                                                      TV[:, 0, n_par(b, k) * 512:n_par(b, k) * 512 + 256],
                                                      f32(KT.hi[:, at:at + 256]), ALU.subtract)
                    else:
                        t = 2 * b + k
                        tv = TV[:, 0, n_par(b, k) * 512:(n_par(b, k) + 1) * 512]
                        ins = nc.gpsimd.tensor_tensor(QT.lo[:, :, t * P:(t + 1) * P],
                                                      tv.rearrange("p (h n) -> p h n", h=4),
                                                      f32(QT.hi[:, :, t * P:(t + 1) * P]), ALU.subtract)
                    ins.then_inc(L["t_lo"], 1)

            def attention(li, g, first_group, last_group):
                L, layer1 = layers[li], li == 1
                units = 8 if layer1 else 16
                pairs = units // 2
                heads = pairs // 2

                for s in steps_of(units, last_group):
                    for event in events_of(li, g, s, first_group, last_group):
                        batch_event(li, *event)
                    if layer1 and (s >= 4 or not first_group) and s % 2 == 0:
                        p = (s - 4) // 2
                        h, b, n = p % heads, p % pairs // heads, g * pairs + p + 1
                        pool.wait_ge(L["o_magic"], n)
                        nc.gpsimd.tensor_tensor(TV[:, 1, 0:T], RP[:, 512:1024], QY[:, 0:T], ALU.add)\
                          .then_inc(L["o_add"], 1)
                        pool.wait_ge(L["o_add"], n)
                        nc.gpsimd.tensor_tensor(OT.hi[:, h:h + 3:2, b * 256:(b + 1) * 256],
                                                TV[:, 1, 0:T].rearrange("p (k n) -> p k n", k=2),
                                                RP[:, 512:1024].rearrange("p (k n) -> p k n", k=2), ALU.subtract)\
                          .then_inc(L["o_q"], 1)
                    for part in (0, 2) if layer1 else (0, 1, 2):
                        if s == SPLITS[li][part] and not last_group:
                            split_part(L, g + 1, part)
                    if s == SPLITS[li][3]:
                        pool.wait_ge(L["wo_hi"], g + 1)
                        nc.gpsimd.tensor_tensor(W.lo[:, O0:SM0], W_raw[:, O0:SM0], f32(W.hi[:, O0:SM0]),
                                                ALU.subtract).then_inc(L["wo_lo"], 1)

            pool.wait_ge(vec_loaded, 16)
            norm_rows(norms[0])
            for part in range(3):
                split_part(layers[0], 0, part)
            pool.wait_ge(ctx_hi, 1)
            nc.gpsimd.tensor_tensor(ctxT.lo[:, :, :], ctx_raw[:, :, :], f32(ctxT.hi[:, :, :]), ALU.subtract)\
              .then_inc(ctx_lo, 1)
            for what, k in FIRST_ORDER:
                batch_event(0, what, (0, 0, k))
            each_group(nc.gpsimd, 4, lambda g, first, last: attention(0, g, first, last))

            def experts(M, n, width):
                def body(i, last_pair):
                    for j in range(2):
                        e = 2 * i + j
                        at = slice(j * EW, j * EW + width)
                        pool.wait_ge(M["w_hi"], e + 1)
                        nc.gpsimd.tensor_tensor(W.lo[:, at], W_raw[:, at], f32(W.hi[:, at]), ALU.subtract)\
                          .then_inc(M["w_lo"], 1)
                each(nc.gpsimd, n // 2, body)

            if stages >= 2:
                norm_rows(norms[1])
                experts(moes[0], E0, EW)
            if stages >= 3:
                norm_rows(norms[2])
                norm_rows(norms[3])
                N = norms[3]
                for part in (0, 2):
                    split_part(layers[1], 0, part)
                for j in (0, 2):
                    pool.wait_ge(N["magic"], j + 1)
                    nc.gpsimd.tensor_tensor(q_sum[0], q_magic[0], q_bf[0], ALU.add).then_inc(N["add"], 1)
                    pool.wait_ge(N["add"], j // 2 + 1)
                    nc.gpsimd.tensor_tensor(xq[j], q_sum[0].rearrange("p (c n) -> p c n", c=HC),
                                            q_magic[0].rearrange("p (c n) -> p c n", c=HC), ALU.subtract)\
                      .then_inc(N["q"], 1)
                for what, k in FIRST_ORDER:
                    batch_event(1, what, (0, 0, k))
                each_group(nc.gpsimd, 8, lambda g, first, last: attention(1, g, first, last))
            if stages >= 4:
                norm_rows(norms[4])
                experts(moes[1], G1, FW)


def kernel(**inputs):
    import concourse.bacc as bacc
    from concourse.bass_utils import run_bass_kernel_spmd

    a = {k: np.asarray(v) for k, v in inputs.items()}

    def chunks(w, rows=P):
        return w.reshape(w.shape[0] // rows, rows, w.shape[1]).transpose(1, 0, 2)

    def cols(w, rows=P):
        w = chunks(w, rows)
        return w.reshape(rows, -1)

    def padded(w):
        return np.concatenate([w, np.zeros((P - w.shape[0], w.shape[1]), w.dtype)])

    groups = []
    for g in range(4):
        kv, q = slice(g * 128, (g + 1) * 128), slice(g * 512, (g + 1) * 512)
        groups.append(np.concatenate([
            cols(np.concatenate([a["L0_xattn_wk_ctx"][:, kv], a["L0_xattn_wv_ctx"][:, kv]], 1)),
            cols(np.concatenate([a["L0_xattn_wk"][:, kv], a["L0_xattn_wv"][:, kv]], 1)),
            cols(a["L0_xattn_wq"][:, q]),
            cols(a["L0_xattn_wo"][q, :]),
            np.zeros((P, SMW), np.float32)], 1))
    smooth = a["L1_xattn_proj_smooth"].reshape(32, P).T
    for g in range(8):
        kv, q = slice(g * 128, (g + 1) * 128), slice(g * 256, (g + 1) * 256)
        kvx = a["L1_xattn_w_kv_x"]
        proj = a["L1_xattn_wproj"].T
        heads = [2 * g, 2 * g + 1, 16 + 2 * g, 17 + 2 * g]
        groups.append(np.concatenate([
            cols(np.concatenate([kvx[0:1024][kv], kvx[1024:2048][kv]], 0).T),
            cols(np.concatenate([a["L1_xattn_wk"][kv], a["L1_xattn_wv"][kv]], 0).T),
            cols(np.concatenate([a["L1_xattn_wq"][q], a["L1_xattn_wqx"][q]], 0).T),
            cols(np.concatenate([proj[h * 128:(h + 1) * 128] for h in heads], 0)),
            smooth[:, heads]], 1))
    experts = [np.concatenate([cols(a["L0_ffn_Win"][e].T), cols(a["L0_ffn_Wout"][e].T)], 1) for e in range(E0)]
    experts1 = []
    for g in range(G1):
        mu = np.zeros((P, H), np.float32)
        mu[g * GS:(g + 1) * GS] = a["L1_ffn_mask_up_w"][g].T
        experts1.append(np.concatenate([
            cols(a["L1_ffn_gate_proj_w"][g].T), cols(a["L1_ffn_up_proj_w"][g].T),
            padded(cols(a["L1_ffn_down_proj_w"][g].T, IH)), mu], 1))

    def col(v):
        return np.broadcast_to(v.reshape(1, 1), (P, 1))

    X1 = "L1_xattn_"
    two = lambda v: v.reshape(2, P).T
    vec = np.concatenate(
        [a["L0_xattn_k_norm_w"].reshape(P, 1)]
        + [a[X1 + n].reshape(P, 1) for n in ("qln_w", "qln_b", "qxln_w", "qxln_b", "kln_w", "kln_b", "kxln_w", "kxln_b")]
        + [two(a[X1 + "ln_w"]), two(a[X1 + "ln_b"])]
        + [two(a[X1 + n]) for n in ("q_in_scale", "qx_in_scale", "k_in_scale", "v_in_scale")]
        + [col(a[X1 + n]) for n in ("wq_scale", "wqx_scale", "wk_scale", "wv_scale", "proj_w_scale", "proj_in_scale")]
        + [np.arange(P, dtype=np.float32).reshape(P, 1), np.full((P, 1), -0.5, np.float32),
           np.full((P, 1), P * RMS_EPS, np.float32), np.full((P, 1), LN_EPS, np.float32)], 1)
    rows = np.broadcast_to(np.stack([a["L0_xattn_q_norm_w"], a["L0_xattn_k_norm_w"]])[None], (P, 2, P))

    f = np.float32
    inv_freq = f(1.0) / f(10000.0) ** (np.arange(0, P, 2, dtype=f) / f(P))
    freqs = np.outer(np.arange(256, dtype=f), inv_freq).astype(f)
    emb = np.concatenate([freqs, freqs], 1)
    sign = np.concatenate([-np.ones(64, f), np.ones(64, f)])
    rope = np.stack([np.cos(emb), np.sin(emb) * sign]).reshape(2, 2, P, P).transpose(2, 0, 1, 3)
    j, i = np.arange(256)[None, None, :], np.arange(256).reshape(2, P).T[:, :, None]
    mask = np.where(j > i, f(NEG), f(0.0))
    falling = np.broadcast_to(np.arange(E0, 0, -1, dtype=f)[None], (P, E0))

    arrays = {
        "x": a["x"].reshape(TT, P, H).transpose(1, 0, 2),
        "ctx": chunks(a["ctx_2048"].reshape(NCTX, H).T),
        "w_groups": np.stack(groups),
        "w_experts0": np.stack(experts),
        "w_experts1": np.stack(experts1),
        "vectors": vec,
        "norm_rows": rows,
        "router0": chunks(a["L0_ffn_Wr"].T),
        "router1": chunks(a["L1_ffn_gate_w"].T),
        "inv_map": np.broadcast_to(a["L1_ffn_inv_map"].reshape(1, NE1), (NE1, NE1)),
        "rope": rope,
        "mask": mask,
        "identity": np.eye(P, dtype=f),
        "falling": falling,
    }
    arrays = {f"in_{k}": np.ascontiguousarray(v) for k, v in arrays.items()}
    nc = bacc.Bacc("TRN2", target_bir_lowering=False, num_devices=1)
    args = [nc.dram_tensor(k, v.shape, mybir.dt.from_np(v.dtype), kind="ExternalInput").ap()
            for k, v in arrays.items()]
    out = nc.dram_tensor("out_x", (P, TT, H), F32, kind="ExternalOutput").ap()
    build(nc, *args, out, STAGES)
    r = run_bass_kernel_spmd(nc, [arrays], core_ids=[0])
    return r.results[0]["out_x"].transpose(1, 0, 2).reshape(2, 256, H)
```
